# Optimizing a Trainium2 kernel written in Bass

```python
import numpy as np
import jax
import jax.numpy as jnp

def _softmax(x, axis=-1):
    return jax.nn.softmax(x, axis=axis)

def _gelu(x):
    return jax.nn.gelu(x, approximate=True)

def _silu(x):
    return jax.nn.silu(x)

def _sigmoid(x):
    return jax.nn.sigmoid(x)

def _layernorm(x, axis=-1, eps=1e-05):
    m = jnp.mean(x, axis=axis, keepdims=True)
    v = jnp.var(x, axis=axis, keepdims=True)
    return (x - m) / jnp.sqrt(v + eps)

def _scatter_add(tgt, idx, src, axis=0):
    return tgt.at[idx].add(src)

def _segment_sum(src, seg, n):
    return jax.ops.segment_sum(src, seg, n)
kernel_name = 'mk_macaron_d1_jaxref_r8_b0e8bf'

def setup_inputs(seed: int=0):
    np.random.seed(seed)
    _w = jnp.asarray

    def _L0_attn_setup():
        import jax, jax.numpy as jnp
        import numpy as np
        D_MODEL = 128
        NHEAD = 16
        HEAD_DIM = D_MODEL // NHEAD
        LN_EPS = 1e-05

        def _retention_scan(v, lam_h):
            B, L, H, DH = v.shape
            a = jnp.broadcast_to(lam_h[None, None, :, None], v.shape)

            def combine(x, y):
                a1, b1 = x
                a2, b2 = y
                return (a1 * a2, a2 * b1 + b2)
            _, states = jax.lax.associative_scan(combine, (a, v), axis=1)
            return states
        key = jax.random.key(seed)
        ks = jax.random.split(key, 6)
        B, L, D = (4, 512, D_MODEL)
        s = 1.0 / np.sqrt(D)
        return {'x': jax.random.normal(ks[0], (B, L, D), jnp.float32), 'Wq': jax.random.normal(ks[1], (D, D), jnp.float32) * s, 'Wv': jax.random.normal(ks[2], (D, D), jnp.float32) * s, 'Wg': jax.random.normal(ks[3], (D, D), jnp.float32) * s, 'Wo': jax.random.normal(ks[4], (D, D), jnp.float32) * s, 'beta': jnp.full((NHEAD,), -0.2, jnp.float32), 'ln_gamma': jnp.ones((D_MODEL,), jnp.float32), 'ln_beta': jnp.zeros((D_MODEL,), jnp.float32)}
    _L0_attn_in = _L0_attn_setup()

    def _L0_ffn_setup():
        import jax, jax.numpy as jnp
        import numpy as np
        B, S, D, M, E, K = (2, 256, 128, 176, 8, 2)
        key = jax.random.key(seed)
        k0, k1, k2, k3, k4 = jax.random.split(key, 5)
        scale = 0.02
        return {'x': jax.random.normal(k0, (B, S, D), dtype=jnp.float32), 'w_gate': jax.random.normal(k1, (D, E), dtype=jnp.float32) * scale, 'w_g': jax.random.normal(k2, (E, D, M), dtype=jnp.float32) * scale, 'w_u': jax.random.normal(k3, (E, D, M), dtype=jnp.float32) * scale, 'w_d': jax.random.normal(k4, (E, M, D), dtype=jnp.float32) * scale}
    _L0_ffn_in = _L0_ffn_setup()
    _d = {'L0_attn_x': _L0_attn_in['x'], 'L0_attn_Wq': _L0_attn_in['Wq'], 'L0_attn_Wv': _L0_attn_in['Wv'], 'L0_attn_Wg': _L0_attn_in['Wg'], 'L0_attn_Wo': _L0_attn_in['Wo'], 'L0_attn_beta': _L0_attn_in['beta'], 'L0_attn_ln_gamma': _L0_attn_in['ln_gamma'], 'L0_attn_ln_beta': _L0_attn_in['ln_beta'], 'L0_ffn_w_gate': _L0_ffn_in['w_gate'], 'L0_ffn_w_g': _L0_ffn_in['w_g'], 'L0_ffn_w_u': _L0_ffn_in['w_u'], 'L0_ffn_w_d': _L0_ffn_in['w_d']}
    _x0 = _d['L0_attn_x']
    _d['L0_attn_x'] = jax.random.normal(jax.random.fold_in(jax.random.key(seed), 1), (8, 512, 128), dtype=_x0.dtype)
    del _x0
    return _d

def reference(L0_attn_x, L0_attn_Wq, L0_attn_Wv, L0_attn_Wg, L0_attn_Wo, L0_attn_beta, L0_attn_ln_gamma, L0_attn_ln_beta, L0_ffn_w_gate, L0_ffn_w_g, L0_ffn_w_u, L0_ffn_w_d):

    def _L0_attn_ref(x, Wq, Wv, Wg, Wo, beta, ln_gamma, ln_beta):
        import jax, jax.numpy as jnp
        import numpy as np
        D_MODEL = 128
        NHEAD = 16
        HEAD_DIM = D_MODEL // NHEAD
        LN_EPS = 1e-05

        def _retention_scan(v, lam_h):
            B, L, H, DH = v.shape
            a = jnp.broadcast_to(lam_h[None, None, :, None], v.shape)

            def combine(x, y):
                a1, b1 = x
                a2, b2 = y
                return (a1 * a2, a2 * b1 + b2)
            _, states = jax.lax.associative_scan(combine, (a, v), axis=1)
            return states
        B, L, D = x.shape
        H, DH = (NHEAD, HEAD_DIM)
        q = (x @ Wq.T).reshape(B, L, H, DH)
        v = (x @ Wv.T).reshape(B, L, H, DH)
        lam_h = jax.nn.sigmoid(beta)
        state = _retention_scan(v, lam_h)
        y = (q * state).reshape(B, L, D)
        mu = jnp.mean(y, axis=-1, keepdims=True)
        var = jnp.mean((y - mu) ** 2, axis=-1, keepdims=True)
        y = (y - mu) * jax.lax.rsqrt(var + LN_EPS) * ln_gamma + ln_beta
        gate = jax.nn.silu(x @ Wg.T)
        y = y * gate
        return y @ Wo.T

    def _L0_ffn_ref(x, w_gate, w_g, w_u, w_d):
        import jax, jax.numpy as jnp
        import numpy as np
        B, S, D, M, E, K = (2, 256, 128, 176, 8, 2)
        scores = x @ w_gate
        topk_scores, topk_idx = jax.lax.top_k(scores, K)
        topk_probs = jax.nn.softmax(topk_scores, axis=-1)
        gating = jnp.sum(jax.nn.one_hot(topk_idx, E, dtype=topk_probs.dtype) * topk_probs[..., None], axis=-2)
        hidden = jax.nn.silu(jnp.einsum('bsd,edm->ebsm', x, w_g)) * jnp.einsum('bsd,edm->ebsm', x, w_u)
        expert_out = jnp.einsum('ebsm,emd->ebsd', hidden, w_d)
        y = jnp.einsum('bse,ebsd->bsd', gating, expert_out)
        return y
    x = L0_attn_x
    x = x + 0.5 * _L0_ffn_ref(_layernorm(x, axis=-1), L0_ffn_w_gate, L0_ffn_w_g, L0_ffn_w_u, L0_ffn_w_d)
    x = x + _L0_attn_ref(_layernorm(x, axis=-1), L0_attn_Wq, L0_attn_Wv, L0_attn_Wg, L0_attn_Wo, L0_attn_beta, L0_attn_ln_gamma, L0_attn_ln_beta)
    x = x + 0.5 * _L0_ffn_ref(_layernorm(x, axis=-1), L0_ffn_w_gate, L0_ffn_w_g, L0_ffn_w_u, L0_ffn_w_d)
    return x

_drawn_inputs = setup_inputs


def setup_inputs(seed=0):
    import zlib

    import numpy as np

    out = dict(_drawn_inputs(seed))
    spreads = {'L0_attn_beta': (-0.20000000298023224, 0.6),
     'L0_attn_ln_gamma': (1.0, 0.2),
     'L0_attn_ln_beta': (0.0, 0.1)}
    factors = {'L0_ffn_w_gate': 8.0, 'L0_ffn_w_g': 8.0, 'L0_ffn_w_u': 8.0, 'L0_ffn_w_d': 8.0}
    for name, (base, spread) in spreads.items():
        noise = np.random.default_rng([zlib.crc32(name.encode()), seed]).standard_normal(out[name].shape)
        drawn = base * np.exp(spread * noise) if base else spread * noise
        out[name] = jnp.asarray(drawn.astype(out[name].dtype))
    for name, factor in factors.items():
        out[name] = (out[name] * factor).astype(out[name].dtype)
    return out
```

```python
from contextlib import ExitStack

import concourse.bass as bass
from concourse import mybir

F32 = mybir.dt.float32
F32R = mybir.dt.float32r
U32 = mybir.dt.uint32
ACT = mybir.ActivationFunctionType
ALU = mybir.AluOpType

P = 128
LN_EPS = 1e-5
EULER = 2.718281828459045
UNITS_AHEAD = 4
HI_LAG = 2
DOWN_LAG = 3
VALUE, QUERY, GATE, OUT = range(4)
SORTING = 6


def macaron_kernel(nc, x_in, w_q, w_v, w_gate_attn, w_o, beta, ln_gamma, ln_beta, w_router, w_g, w_u, w_d, out):
    GROUPS, TOKENS, D = x_in.shape
    EXPERTS, _, HIDDEN = w_g.shape
    HEADS = beta.shape[0]
    TILES = TOKENS // P
    BLOCKS = EXPERTS * HIDDEN // P
    PER_EXPERT = P // EXPERTS
    UNITS = 2 * GROUPS
    HEAD_DIM = D // HEADS
    assert D == P and HIDDEN == PER_EXPERT * BLOCKS and TOKENS == 512

    def final_unit(g):
        return UNITS_AHEAD + 2 * g if g < GROUPS - UNITS_AHEAD else GROUPS + g

    def wait(eng, sem, count):
        if not isinstance(count, int) or count > 0:
            eng.wait_ge(sem, count)

    with ExitStack() as ctx:
        def sb(name, shape, dt=F32):
            return ctx.enter_context(nc.sbuf_tensor(name, shape, dt))

        def bank(name):
            return ctx.enter_context(nc.psum_tensor(name, [P, 512], F32))

        def sem(name):
            return ctx.enter_context(nc.semaphore(name))

        x = sb("x", [P, GROUPS * TOKENS])

        gate_raw = sb("gate_raw", [P, EXPERTS * HIDDEN])
        up_raw = sb("up_raw", [P, EXPERTS * HIDDEN])
        down_raw = sb("down_raw", [P, EXPERTS * HIDDEN])
        gate_hi, gate_lo, up_hi, up_lo, down_hi, down_lo = (
            sb(n, [P, BLOCKS, P], F32R) for n in ("gate_hi", "gate_lo", "up_hi", "up_lo", "down_hi", "down_lo"))
        router_raw = sb("router_raw", [P, EXPERTS])
        router_hi = sb("router_hi", [P, EXPERTS], F32R)
        router_lo = sb("router_lo", [P, EXPERTS], F32R)
        attn_raw = sb("attn_raw", [P, 4, P])
        attn_w_hi = sb("attn_w_hi", [P, 4, P], F32R)
        attn_w_lo = sb("attn_w_lo", [P, 4, P], F32R)
        beta_col = sb("beta_col", [P, 1])
        decay = sb("decay", [P, 1])
        gamma_col = sb("gamma_col", [P, 1])
        shift_col = sb("shift_col", [P, 1])

        ident = sb("ident", [P, P])
        minus_half = sb("minus_half", [P, TILES])
        euler = sb("euler", [P, TILES])
        expert_id = sb("expert_id", [P, EXPERTS])

        act_pulse = sb("act_pulse", [P, 3])
        dve_pulse = sb("dve_pulse", [P, 7])

        xt_hi = [sb(f"xt_hi{i}", [P, TOKENS], F32R) for i in range(2)]
        xt_lo = [sb(f"xt_lo{i}", [P, TOKENS], F32R) for i in range(2)]
        gates = [sb(f"gates{i}", [P, TOKENS]) for i in range(2)]
        silu = sb("silu", [P, 2, TOKENS])
        hidden = sb("hidden", [P, BLOCKS, TOKENS])
        hidden_hi = sb("hidden_hi", [P, BLOCKS, TOKENS], F32R)
        hidden_lo = sb("hidden_lo", [P, BLOCKS, TOKENS], F32R)
        half_down = sb("half_down", [P, TOKENS])

        prep_xn = sb("prep_xn", [P, TOKENS])
        prep_bn = sb("prep_bn", [P, TILES, 6])
        prep_mv = sb("prep_mv", [P, TILES, 2])
        prep_ve = sb("prep_ve", [P, TILES])
        prep_nm = sb("prep_nm", [P, TILES])
        prep_rstd = sb("prep_rstd", [P, TILES])
        prep_bias = sb("prep_bias", [P, TILES])
        scores = sb("scores", [P, TILES, EXPERTS])
        sorted_scores = sb("sorted_scores", [P, TILES, 8])
        sorted_ids = sb("sorted_ids", [P, TILES, 8], U32)
        top_ids = sb("top_ids", [P, TILES, 2])
        is_top = sb("is_top", [P, TILES, 2, EXPERTS])
        top_gap = sb("top_gap", [P, TILES])
        top_exp = sb("top_exp", [P, TILES])
        top_sum = sb("top_sum", [P, TILES])
        top_prob = sb("top_prob", [P, TILES, 2])
        top_gate = sb("top_gate", [P, TILES, 2, EXPERTS])
        gates_tok = sb("gates_tok", [P, TILES, EXPERTS, PER_EXPERT])

        attn_xn = sb("attn_xn", [P, TOKENS])
        attn_bn = sb("attn_bn", [P, TILES, 6])
        attn_mv = sb("attn_mv", [P, TILES, 2])
        attn_ve = sb("attn_ve", [P, TILES])
        attn_nm = sb("attn_nm", [P, TILES])
        attn_rstd = sb("attn_rstd", [P, TILES])
        attn_bias = sb("attn_bias", [P, TILES])
        attn_xt_hi = sb("attn_xt_hi", [P, TOKENS], F32R)
        attn_xt_lo = sb("attn_xt_lo", [P, TOKENS], F32R)
        state = sb("state", [P, TOKENS])
        y = sb("y", [P, TOKENS])
        y_bn = sb("y_bn", [P, TILES, 6])
        y_mv = sb("y_mv", [P, TILES, 2])
        y_ve = sb("y_ve", [P, TILES])
        y_nm = sb("y_nm", [P, TILES])
        y_rstd = sb("y_rstd", [P, TILES])
        y_bias = sb("y_bias", [P, TILES])
        y_norm = sb("y_norm", [P, TOKENS])
        attn_gate = sb("attn_gate", [P, TOKENS])
        z_affine = sb("z_affine", [P, TOKENS])
        z = sb("z", [P, TOKENS])
        z_hi = sb("z_hi", [P, TOKENS], F32R)
        z_lo = sb("z_lo", [P, TOKENS], F32R)
        attn_out = sb("attn_out", [P, TOKENS])

        gate_ps = [bank(f"gate_ps{i}") for i in range(2)]
        up_ps = [bank(f"up_ps{i}") for i in range(2)]
        down_ps = bank("down_ps")
        prep_ps = bank("prep_ps")
        attn_a = bank("attn_a")
        attn_b = bank("attn_b")

        x0_loaded = sem("x0_loaded")
        x_loaded = sem("x_loaded")
        router_loaded = sem("router_loaded")
        gate_loaded = sem("gate_loaded")
        up_loaded = sem("up_loaded")
        down_loaded = sem("down_loaded")
        attn_loaded = sem("attn_loaded")
        columns_loaded = sem("columns_loaded")
        ident_zero = sem("ident_zero")
        ident_ready = sem("ident_ready")
        consts_ready = sem("consts_ready")
        router_hi_ready = sem("router_hi_ready")
        router_ready = sem("router_ready")
        expert_hi_ready = sem("expert_hi_ready")
        expert_ready = sem("expert_ready")
        decay_ready = sem("decay_ready")
        attn_wt_ready = sem("attn_wt_ready")
        attn_w_hi_ready = sem("attn_w_hi_ready")
        attn_w_ready = sem("attn_w_ready")
        gate_ready = sem("gate_ready")
        up_ready = sem("up_ready")
        silu_done = sem("silu_done")
        product_done = sem("product_done")
        gated_done = sem("gated_done")
        hidden_hi_done = sem("hidden_hi_done")
        hidden_lo_done = sem("hidden_lo_done")
        down_done = sem("down_done")
        down_copied = sem("down_copied")
        resid_t_ready = sem("resid_t_ready")
        resid_done = sem("resid_done")
        prep_bn_done = sem("prep_bn_done")
        prep_mv_done = sem("prep_mv_done")
        prep_stats_done = sem("prep_stats_done")
        prep_rstd_done = sem("prep_rstd_done")
        prep_scale_done = sem("prep_scale_done")
        prep_norm_done = sem("prep_norm_done")
        prep_t_ready = sem("prep_t_ready")
        prep_hi_done = sem("prep_hi_done")
        prep_lo_done = sem("prep_lo_done")
        scores_ready = sem("scores_ready")
        scores_copied = sem("scores_copied")
        sorted_done = sem("sorted_done")
        ids_done = sem("ids_done")
        gap_done = sem("gap_done")
        exp_done = sem("exp_done")
        top_ids_done = sem("top_ids_done")
        is_top_done = sem("is_top_done")
        sum_done = sem("sum_done")
        first_prob_done = sem("first_prob_done")
        probs_done = sem("probs_done")
        top_gate_done = sem("top_gate_done")
        gates_tok_done = sem("gates_tok_done")
        gates_t_ready = sem("gates_t_ready")
        gates_done = sem("gates_done")
        attn_bn_done = sem("attn_bn_done")
        attn_mv_done = sem("attn_mv_done")
        attn_stats_done = sem("attn_stats_done")
        attn_rstd_done = sem("attn_rstd_done")
        attn_scale_done = sem("attn_scale_done")
        attn_norm_done = sem("attn_norm_done")
        attn_t_ready = sem("attn_t_ready")
        attn_hi_done = sem("attn_hi_done")
        attn_lo_done = sem("attn_lo_done")
        value_ready = sem("value_ready")
        query_ready = sem("query_ready")
        attn_gate_ready = sem("attn_gate_ready")
        state_done = sem("state_done")
        attn_gate_done = sem("attn_gate_done")
        y_done = sem("y_done")
        y_t_ready = sem("y_t_ready")
        y_bn_done = sem("y_bn_done")
        y_mv_done = sem("y_mv_done")
        y_stats_done = sem("y_stats_done")
        y_rstd_done = sem("y_rstd_done")
        y_scale_done = sem("y_scale_done")
        y_norm_done = sem("y_norm_done")
        z_t_ready = sem("z_t_ready")
        z_affine_done = sem("z_affine_done")
        z_done = sem("z_done")
        z_hi_done = sem("z_hi_done")
        z_lo_done = sem("z_lo_done")
        attn_out_ready = sem("attn_out_ready")
        attn_out_copied = sem("attn_out_copied")
        attn_resid_t_ready = sem("attn_resid_t_ready")
        attn_resid_done = sem("attn_resid_done")
        stored = sem("stored")

        def run_slots(eng, slot):
            slot(n=0, odd=0, prep=1)
            slot(n=1, odd=1, prep=2, done=0)
            with eng.Fori(0, 4) as i:
                first = 1 // (i + 1)
                even_done = nc.s_assert_within((i + 2) - first, 1, 5, skip_runtime_bounds_check_because="i is in 0..3")
                odd_done = nc.s_assert_within((i + 3 * first) - 1, 0, 2, skip_runtime_bounds_check_because="i is in 0..3")
                slot(n=2 * i + 2, odd=0, prep=i + 3, attn=i, done=even_done)
                slot(n=2 * i + 3, odd=1, prep=i, left=i, done=odd_done)
            slot(n=10, odd=0, prep=7, attn=4, done=6)
            slot(n=11, odd=1, prep=4, attn=5, left=4, done=3)
            slot(n=12, odd=0, prep=5, attn=6, left=5, done=7)
            slot(n=13, odd=1, prep=6, attn=7, left=6, done=4)
            slot(n=14, odd=0, prep=7, left=7, done=5)
            slot(n=15, odd=1, done=6)

        block = ctx.enter_context(nc.Block())

        @block.sync
        def _(sp):
            xv = x[:].rearrange("p (g t d) -> p g t d", t=TILES, d=D)
            sp.dma_start(xv[:, 0], x_in[0].rearrange("(t p) d -> p t d", p=P)).then_inc(x0_loaded, 16)
            sp.dma_start(router_raw[:], w_router).then_inc(router_loaded, 16)
            sp.dma_start(gate_raw[:].rearrange("d (e m) -> d e m", e=EXPERTS),
                         w_g.rearrange("e d m -> d e m")).then_inc(gate_loaded, 16)
            sp.dma_start(up_raw[:].rearrange("d (e m) -> d e m", e=EXPERTS),
                         w_u.rearrange("e d m -> d e m")).then_inc(up_loaded, 16)
            for g in range(1, GROUPS):
                sp.dma_start(xv[:, g], x_in[g].rearrange("(t p) d -> p t d", p=P)).then_inc(x_loaded, 16)
                if g == 1:
                    sp.dma_start(down_raw[:], w_d.rearrange("e m d -> (e m) d").rearrange(
                        "(p b) d -> p (b d)", b=BLOCKS)).then_inc(down_loaded, 16)
            for g in range(GROUPS):
                sp.wait_ge(resid_done, final_unit(g) + 1)
                sp.dma_start(out[g].rearrange("(t p) d -> p t d", p=P), xv[:, g]).then_inc(stored, 16)
            sp.wait_ge(stored, 16 * GROUPS)

        @block.gpsimd
        def _(pool):
            nc.gpsimd.memset(ident[:], 0.0).then_inc(ident_zero, 1)
            pool.wait_ge(ident_zero, 1)
            nc.gpsimd.affine_select(out=ident[:], in_=ident[:], compare_op=ALU.not_equal, fill=1.0, base=0,
                                    pattern=[[-1, P]], channel_multiplier=1).then_inc(ident_ready, 1)
            nc.gpsimd.memset(minus_half[:], -0.5)
            nc.gpsimd.memset(euler[:], EULER)
            for e in range(EXPERTS):
                last = nc.gpsimd.memset(expert_id[:, e:e + 1], float(e))
            last.then_inc(consts_ready, 1)
            pool.wait_ge(consts_ready, 1)

            def scale_of(ve, nm, rstd, bias, stats_done, rstd_done, scale_done, count):
                pool.wait_ge(stats_done, count)
                nc.gpsimd.tensor_tensor(rstd[:], ve[:], minus_half[:], ALU.pow).then_inc(rstd_done, 1)
                pool.wait_ge(rstd_done, count)
                nc.gpsimd.tensor_tensor(bias[:], nm[:], rstd[:], ALU.mult).then_inc(scale_done, 1)

            def prep_scale(p):
                scale_of(prep_ve, prep_nm, prep_rstd, prep_bias, prep_stats_done, prep_rstd_done, prep_scale_done, p + 1)

            def top_exponential(p):
                pool.wait_ge(gap_done, p + 1)
                nc.gpsimd.tensor_tensor(top_exp[:], euler[:], top_gap[:], ALU.pow).then_inc(exp_done, 1)

            def slot(n, odd, prep=None, attn=None, left=None, done=None):
                for b in range(BLOCKS):
                    if b == 0 and attn is not None:
                        scale_of(attn_ve, attn_nm, attn_rstd, attn_bias, attn_stats_done, attn_rstd_done,
                                 attn_scale_done, attn + 1)
                    if b == 2 and prep is not None:
                        prep_scale(n + 1)
                    if b == 5 and attn is not None:
                        scale_of(y_ve, y_nm, y_rstd, y_bias, y_stats_done, y_rstd_done, y_scale_done, attn + 1)
                    if b == 6 and prep is not None:
                        top_exponential(n + 1)
                    if b == 8 and attn is not None:
                        pool.wait_ge(z_affine_done, attn + 1)
                        pool.wait_ge(attn_gate_done, attn + 1)
                        nc.gpsimd.tensor_tensor(z[:], z_affine[:], attn_gate[:], ALU.mult).then_inc(z_done, 1)
                    if b == 0:
                        pool.wait_ge(gates_done, n + 1)
                    pool.wait_ge(product_done, BLOCKS * n + b + 1)
                    nc.gpsimd.tensor_tensor(hidden[:, b, :], hidden[:, b, :], gates[odd][:],
                                            ALU.mult).then_inc(gated_done, 1)

            prep_scale(0)
            top_exponential(0)
            run_slots(pool, slot)

        @block.scalar
        def _(act):
            act.dma_start(beta_col[:], beta.rearrange("(h o) -> h o", o=1).broadcast_to(
                [HEADS, HEAD_DIM])).then_inc(columns_loaded, 16)
            act.dma_start(gamma_col[:], ln_gamma.rearrange("(d o) -> d o", o=1)).then_inc(columns_loaded, 16)
            act.dma_start(shift_col[:], ln_beta.rearrange("(d o) -> d o", o=1)).then_inc(columns_loaded, 16)
            for k, w in ((VALUE, w_v), (QUERY, w_q), (GATE, w_gate_attn), (OUT, w_o)):
                act.dma_start(attn_raw[:, k, :], w).then_inc(attn_loaded, 16)
            act.wait_ge(columns_loaded, 48)
            nc.scalar.activation(decay[:], beta_col[:], ACT.Sigmoid).then_inc(decay_ready, 1)

            def normalise(dst, src_tile, rstd, bias, scale_done, norm_done, count, pulse):
                act.wait_ge(scale_done, count)
                nc.scalar.activation(act_pulse[:, pulse:pulse + 1], minus_half[:, 0:1], ACT.Copy)
                for t in range(TILES):
                    last = nc.scalar.activation(dst[:, t * P:(t + 1) * P], src_tile(t), ACT.Identity,
                                                bias=bias[:, t:t + 1], scale=rstd[:, t:t + 1])
                last.then_inc(norm_done, 1)

            def prep_norm(p, g):
                wait(act, prep_t_ready, p)
                normalise(prep_xn, lambda t: x[:, bass.ds(g * TOKENS + t * P, P)], prep_rstd, prep_bias,
                          prep_scale_done, prep_norm_done, p + 1, pulse=0)

            def prep_hi(p, odd):
                act.wait_ge(prep_t_ready, p + 1)
                nc.scalar.activation(xt_hi[odd][:], prep_ps[:], ACT.Copy).then_inc(prep_hi_done, 1)

            def gates_copy(p, odd):
                act.wait_ge(gates_t_ready, p + 1)
                nc.scalar.activation(gates[odd][:], prep_ps[:], ACT.Copy).then_inc(gates_done, 1)

            def hidden_split(q, b):
                act.wait_ge(gated_done, q + 1)
                wait(act, down_done, q + 1 - BLOCKS)
                nc.scalar.activation(hidden_hi[:, b, :], hidden[:, b, :], ACT.Copy).then_inc(hidden_hi_done, 1)

            def copy_down(n):
                act.wait_ge(down_done, BLOCKS * (n + 1))
                wait(act, resid_t_ready, n)
                nc.scalar.activation(half_down[:], down_ps[:], ACT.Copy, scale=0.5).then_inc(down_copied, 1)

            def slot(n, odd, prep=None, attn=None, left=None, done=None):
                for b in range(BLOCKS):
                    if b == 0 and left is not None:
                        act.wait_ge(attn_out_ready, left + 1)
                        nc.scalar.activation(attn_out[:], attn_a[:], ACT.Copy).then_inc(attn_out_copied, 1)
                    if b == 2 and attn is not None:
                        wait(act, attn_t_ready, attn)
                        normalise(attn_xn, lambda t: x[:, bass.ds(attn * TOKENS + t * P, P)], attn_rstd, attn_bias,
                                  attn_scale_done, attn_norm_done, attn + 1, pulse=1)
                    if b == 3 and done is not None:
                        copy_down(n - 1)
                    if b == 3 and attn is not None:
                        act.wait_ge(attn_t_ready, attn + 1)
                        nc.scalar.activation(attn_xt_hi[:], attn_a[:], ACT.Copy).then_inc(attn_hi_done, 1)
                    if b == 4 and prep is not None:
                        prep_norm(n + 1, prep)
                    if b == 5 and prep is not None:
                        prep_hi(n + 1, 1 - odd)
                    if b == 5 and attn is not None:
                        act.wait_ge(attn_gate_ready, attn + 1)
                        nc.scalar.activation(attn_gate[:], attn_b[:], ACT.Silu).then_inc(attn_gate_done, 1)
                    if b == 7 and attn is not None:
                        normalise(y_norm, lambda t: attn_a[:, t * P:(t + 1) * P], y_rstd, y_bias,
                                  y_scale_done, y_norm_done, attn + 1, pulse=2)
                    if b == 8 and attn is not None:
                        act.wait_ge(z_t_ready, attn + 1)
                        nc.scalar.activation(z_affine[:], attn_b[:], ACT.Identity, bias=shift_col[:, 0:1],
                                             scale=gamma_col[:, 0:1]).then_inc(z_affine_done, 1)
                    if b == 9 and prep is not None:
                        gates_copy(n + 1, 1 - odd)
                    if b == 10 and attn is not None:
                        act.wait_ge(z_done, attn + 1)
                        nc.scalar.activation(z_hi[:], z[:], ACT.Copy).then_inc(z_hi_done, 1)
                    q = BLOCKS * n + b
                    act.wait_ge(gate_ready, q + 1)
                    wait(act, product_done, q - 1)
                    nc.scalar.activation(silu[:, (odd + b) % 2, :], gate_ps[(odd + b) % 2][:],
                                         ACT.Silu).then_inc(silu_done, 1)
                    if not isinstance(n, int) or n > 0 or b >= HI_LAG:
                        hidden_split(q - HI_LAG, (b - HI_LAG) % BLOCKS)

            act.wait_ge(x0_loaded, 16)
            act.wait_ge(consts_ready, 1)
            prep_norm(0, 0)
            act.wait_ge(router_loaded, 16)
            nc.scalar.activation(router_hi[:], router_raw[:], ACT.Copy).then_inc(router_hi_ready, 1)
            prep_hi(0, 0)
            for raw, hi, loaded, strided in ((gate_raw, gate_hi, gate_loaded, True), (up_raw, up_hi, up_loaded, True),
                                             (down_raw, down_hi, down_loaded, False)):
                act.wait_ge(loaded, 16)
                src = raw[:].rearrange("k (p b) -> k b p", b=BLOCKS) if strided else \
                    raw[:].rearrange("k (b d) -> k b d", b=BLOCKS)
                nc.scalar.activation(hi[:], src, ACT.Copy).then_inc(expert_hi_ready, 1)
            gates_copy(0, 0)
            act.wait_ge(attn_wt_ready, 1)
            nc.scalar.activation(attn_w_hi[:].rearrange("p k c -> p (k c)"), attn_a[:], ACT.Copy).then_inc(
                attn_w_hi_ready, 1)
            run_slots(act, slot)
            for b in range(BLOCKS - HI_LAG, BLOCKS):
                hidden_split(BLOCKS * (UNITS - 1) + b, b)
            copy_down(UNITS - 1)

        @block.vector
        def _(dve):
            def stand_in(pulse):
                nc.vector.memset(dve_pulse[:, pulse:pulse + 1], 0.0)

            def moments(src_tile, bn, mv, ve, nm, bn_done, mv_done, stats_done, count, pulse):
                stand_in(pulse + 1)
                for t in range(TILES):
                    last = nc.vector.bn_stats(bn[:, t, :], src_tile(t))
                last.then_inc(bn_done, 1)
                dve.wait_ge(bn_done, count)
                stand_in(pulse)
                for t in range(TILES):
                    last = nc.vector.bn_aggr(mv[:, t, :], bn[:, t, :])
                last.then_inc(mv_done, 1)
                dve.wait_ge(mv_done, count)
                nc.vector.tensor_scalar(ve[:], mv[:, :, 1], LN_EPS, None, ALU.add)
                nc.vector.tensor_scalar(nm[:], mv[:, :, 0], -1.0, None, ALU.mult).then_inc(stats_done, 1)

            def prep_moments(p, g):
                moments(lambda t: x[:, bass.ds(g * TOKENS + t * P, P)], prep_bn, prep_mv, prep_ve, prep_nm,
                        prep_bn_done, prep_mv_done, prep_stats_done, p + 1, pulse=0)

            def prep_lo(p, odd):
                dve.wait_ge(prep_hi_done, p + 1)
                nc.vector.tensor_tensor(xt_lo[odd][:], prep_ps[:], xt_hi[odd][:].bitcast(F32),
                                        ALU.subtract).then_inc(prep_lo_done, 1)

            def top_two(p):
                dve.wait_ge(scores_ready, p + 1)
                nc.vector.tensor_copy(scores[:].rearrange("p t e -> p (t e)"),
                                      prep_ps[:, 0:TILES * EXPERTS]).then_inc(scores_copied, 1)
                dve.wait_ge(scores_copied, p + 1)
                stand_in(SORTING)
                for t in range(TILES):
                    last = nc.vector.max(sorted_scores[:, t, :], scores[:, t, :])
                last.then_inc(sorted_done, 1)
                dve.wait_ge(sorted_done, p + 1)
                nc.vector.tensor_tensor(top_gap[:], sorted_scores[:, :, 1], sorted_scores[:, :, 0],
                                        ALU.subtract).then_inc(gap_done, 1)
                for t in range(TILES):
                    last = nc.vector.max_index(sorted_ids[:, t, :], sorted_scores[:, t, :], scores[:, t, :])
                last.then_inc(ids_done, 1)
                dve.wait_ge(ids_done, p + 1)
                nc.vector.tensor_copy(top_ids[:], sorted_ids[:, :, 0:2]).then_inc(top_ids_done, 1)
                dve.wait_ge(top_ids_done, p + 1)
                shape = [P, TILES, 2, EXPERTS]
                nc.vector.tensor_tensor(is_top[:], expert_id[:].unsqueeze(1).unsqueeze(1).broadcast_to(shape),
                                        top_ids[:].unsqueeze(3).broadcast_to(shape),
                                        ALU.is_equal).then_inc(is_top_done, 1)

            def gate_rows(p):
                dve.wait_ge(exp_done, p + 1)
                nc.vector.tensor_scalar(top_sum[:], top_exp[:], 1.0, None, ALU.add).then_inc(sum_done, 1)
                dve.wait_ge(sum_done, p + 1)
                nc.vector.reciprocal(top_prob[:, :, 0], top_sum[:]).then_inc(first_prob_done, 1)
                dve.wait_ge(first_prob_done, p + 1)
                nc.vector.tensor_tensor(top_prob[:, :, 1], top_prob[:, :, 0], top_exp[:],
                                        ALU.mult).then_inc(probs_done, 1)
                dve.wait_ge(probs_done, p + 1)
                dve.wait_ge(is_top_done, p + 1)
                nc.vector.tensor_tensor(top_gate[:], is_top[:],
                                        top_prob[:].unsqueeze(3).broadcast_to([P, TILES, 2, EXPERTS]),
                                        ALU.mult).then_inc(top_gate_done, 1)
                dve.wait_ge(top_gate_done, p + 1)
                shape = [P, TILES, EXPERTS, PER_EXPERT]
                nc.vector.tensor_tensor(gates_tok[:], top_gate[:, :, 0, :].unsqueeze(3).broadcast_to(shape),
                                        top_gate[:, :, 1, :].unsqueeze(3).broadcast_to(shape),
                                        ALU.add).then_inc(gates_tok_done, 1)

            def hidden_rest(q, b):
                dve.wait_ge(hidden_hi_done, q + 1)
                nc.vector.tensor_tensor(hidden_lo[:, b, :], hidden[:, b, :], hidden_hi[:, b, :].bitcast(F32),
                                        ALU.subtract).then_inc(hidden_lo_done, 1)

            def add_unit(n, g):
                dve.wait_ge(resid_t_ready, n + 1)
                xg = x[:, bass.ds(g * TOKENS, TOKENS)]
                nc.vector.tensor_tensor(xg, prep_ps[:], xg, ALU.add).then_inc(resid_done, 1)

            def slot(n, odd, prep=None, attn=None, left=None, done=None):
                for b in range(BLOCKS):
                    if b == 0 and attn is not None:
                        dve.wait_ge(resid_done, n - 1)
                        moments(lambda t: x[:, bass.ds(attn * TOKENS + t * P, P)], attn_bn, attn_mv, attn_ve, attn_nm,
                                attn_bn_done, attn_mv_done, attn_stats_done, attn + 1, pulse=2)
                    if b == 1 and left is not None:
                        dve.wait_ge(attn_resid_t_ready, left + 1)
                        xg = x[:, bass.ds(left * TOKENS, TOKENS)]
                        nc.vector.tensor_tensor(xg, attn_b[:], xg, ALU.add).then_inc(attn_resid_done, 1)
                    if b == 2 and prep is not None:
                        if left is not None:
                            dve.wait_ge(attn_resid_done, left + 1)
                        prep_moments(n + 1, prep)
                    if b == 3 and attn is not None:
                        dve.wait_ge(attn_hi_done, attn + 1)
                        nc.vector.tensor_tensor(attn_xt_lo[:], attn_a[:], attn_xt_hi[:].bitcast(F32),
                                                ALU.subtract).then_inc(attn_lo_done, 1)
                    if b == 4 and done is not None:
                        add_unit(n - 1, done)
                    if b == 4 and attn is not None:
                        dve.wait_ge(value_ready, attn + 1)
                        nc.vector.tensor_tensor_scan(state[:], decay[:, 0:1].to_broadcast([P, TOKENS]), attn_b[:],
                                                     0.0, ALU.mult, ALU.add).then_inc(state_done, 1)
                        dve.wait_ge(state_done, attn + 1)
                        dve.wait_ge(query_ready, attn + 1)
                        nc.vector.tensor_tensor(y[:], attn_a[:], state[:], ALU.mult).then_inc(y_done, 1)
                    if b == 5 and attn is not None:
                        dve.wait_ge(y_t_ready, attn + 1)
                        moments(lambda t: attn_a[:, t * P:(t + 1) * P], y_bn, y_mv, y_ve, y_nm,
                                y_bn_done, y_mv_done, y_stats_done, attn + 1, pulse=4)
                    if b == 5 and prep is not None:
                        prep_lo(n + 1, 1 - odd)
                    if b == 6 and prep is not None:
                        top_two(n + 1)
                    if b == 8 and prep is not None:
                        gate_rows(n + 1)
                    if b == 10 and attn is not None:
                        dve.wait_ge(z_hi_done, attn + 1)
                        nc.vector.tensor_tensor(z_lo[:], z[:], z_hi[:].bitcast(F32),
                                                ALU.subtract).then_inc(z_lo_done, 1)
                    q = BLOCKS * n + b
                    dve.wait_ge(silu_done, q + 1)
                    dve.wait_ge(up_ready, q + 1)
                    nc.vector.tensor_tensor(hidden[:, b, :], up_ps[(odd + b) % 2][:], silu[:, (odd + b) % 2, :],
                                            ALU.mult).then_inc(product_done, 1)
                    if not isinstance(n, int) or n > 0 or b >= HI_LAG:
                        hidden_rest(q - HI_LAG, (b - HI_LAG) % BLOCKS)

            dve.wait_ge(x0_loaded, 16)
            prep_moments(0, 0)
            prep_lo(0, 0)
            dve.wait_ge(router_hi_ready, 1)
            nc.vector.tensor_tensor(router_lo[:], router_raw[:], router_hi[:].bitcast(F32),
                                    ALU.subtract).then_inc(router_ready, 1)
            dve.wait_ge(consts_ready, 1)
            for k, (raw, hi, lo, strided) in enumerate(((gate_raw, gate_hi, gate_lo, True), (up_raw, up_hi, up_lo, True),
                                                        (down_raw, down_hi, down_lo, False))):
                dve.wait_ge(expert_hi_ready, k + 1)
                src = raw[:].rearrange("k (p b) -> k b p", b=BLOCKS) if strided else \
                    raw[:].rearrange("k (b d) -> k b d", b=BLOCKS)
                nc.vector.tensor_tensor(lo[:], src, hi[:].bitcast(F32), ALU.subtract).then_inc(expert_ready, 1)
                if k == 0:
                    top_two(0)
                if k == 1:
                    gate_rows(0)
            dve.wait_ge(attn_w_hi_ready, 1)
            nc.vector.tensor_tensor(attn_w_lo[:].rearrange("p k c -> p (k c)"), attn_a[:],
                                    attn_w_hi[:].rearrange("p k c -> p (k c)").bitcast(F32),
                                    ALU.subtract).then_inc(attn_w_ready, 1)
            dve.wait_ge(x_loaded, 16 * (GROUPS - 1))
            dve.wait_ge(decay_ready, 1)
            run_slots(dve, slot)
            for b in range(BLOCKS - HI_LAG, BLOCKS):
                hidden_rest(BLOCKS * (UNITS - 1) + b, b)
            add_unit(UNITS - 1, GROUPS - 1)

        @block.tensor
        def _(pe):
            def product(dst, w_hi, w_lo, v_hi, v_lo, start=True, stop=True):
                nc.tensor.matmul(dst, w_hi, v_hi, start=start, stop=False)
                nc.tensor.matmul(dst, w_hi, v_lo, start=False, stop=False)
                return nc.tensor.matmul(dst, w_lo, v_hi, start=False, stop=stop)

            def transposes(dst, src):
                for t in range(TILES):
                    last = nc.tensor.transpose(dst[:, t * P:(t + 1) * P], src[:, t * P:(t + 1) * P], ident[:])
                return last

            def prep_transpose(p):
                wait(pe, gates_done, p)
                wait(pe, resid_done, p - 1)
                pe.wait_ge(prep_norm_done, p + 1)
                transposes(prep_ps, prep_xn).then_inc(prep_t_ready, 1)

            def router(p, odd):
                pe.wait_ge(prep_lo_done, p + 1)
                for t in range(TILES):
                    cols = slice(t * P, (t + 1) * P)
                    dst = prep_ps[:, t * EXPERTS:(t + 1) * EXPERTS]
                    last = product(dst, xt_hi[odd][:, cols], xt_lo[odd][:, cols], router_hi[:], router_lo[:])
                last.then_inc(scores_ready, 1)

            def gates_transpose(p):
                pe.wait_ge(scores_copied, p + 1)
                pe.wait_ge(gates_tok_done, p + 1)
                transposes(prep_ps, gates_tok[:].rearrange("p t e r -> p (t e r)")).then_inc(gates_t_ready, 1)

            def down(q, b, n):
                pe.wait_ge(hidden_lo_done, q + 1)
                if b == 0:
                    wait(pe, down_copied, n)
                product(down_ps[:], down_hi[:, b, :], down_lo[:, b, :], hidden_hi[:, b, :], hidden_lo[:, b, :],
                        start=b == 0, stop=b == BLOCKS - 1).then_inc(down_done, 1)

            def attn_product(dst, k):
                return product(dst[:], attn_w_hi[:, k, :], attn_w_lo[:, k, :], attn_xt_hi[:], attn_xt_lo[:])

            def resid_transpose(n):
                wait(pe, gates_done, n + 2 if not isinstance(n, int) or n + 1 < UNITS else UNITS)
                pe.wait_ge(down_copied, n + 1)
                transposes(prep_ps, half_down).then_inc(resid_t_ready, 1)

            def slot(n, odd, prep=None, attn=None, left=None, done=None):
                pe.wait_ge(prep_lo_done, n + 1)
                for b in range(BLOCKS):
                    q = BLOCKS * n + b
                    wait(pe, silu_done, q - 1)
                    product(gate_ps[(odd + b) % 2][:], gate_hi[:, b, :], gate_lo[:, b, :],
                            xt_hi[odd][:], xt_lo[odd][:]).then_inc(gate_ready, 1)
                    if isinstance(n, int) and n == 0 and b == 0:
                        pe.wait_ge(expert_ready, 2)
                    wait(pe, product_done, q - 1)
                    product(up_ps[(odd + b) % 2][:], up_hi[:, b, :], up_lo[:, b, :],
                            xt_hi[odd][:], xt_lo[odd][:]).then_inc(up_ready, 1)
                    if isinstance(n, int) and n == 0 and b == DOWN_LAG:
                        pe.wait_ge(expert_ready, 3)
                    if not isinstance(n, int) or n > 0 or b >= DOWN_LAG:
                        down(q - DOWN_LAG, (b - DOWN_LAG) % BLOCKS, n)
                    if b == 0 and left is not None:
                        pe.wait_ge(attn_out_copied, left + 1)
                        transposes(attn_b, attn_out).then_inc(attn_resid_t_ready, 1)
                    if b == 2 and attn is not None:
                        wait(pe, attn_out_copied, attn)
                        pe.wait_ge(attn_norm_done, attn + 1)
                        transposes(attn_a, attn_xn).then_inc(attn_t_ready, 1)
                    if b == 3 and done is not None:
                        resid_transpose(n - 1)
                    if b == 3 and attn is not None:
                        wait(pe, attn_resid_done, attn)
                        pe.wait_ge(attn_lo_done, attn + 1)
                        attn_product(attn_b, VALUE).then_inc(value_ready, 1)
                        attn_product(attn_a, QUERY).then_inc(query_ready, 1)
                    if b == 4 and prep is not None:
                        prep_transpose(n + 1)
                    if b == 4 and attn is not None:
                        pe.wait_ge(state_done, attn + 1)
                        attn_product(attn_b, GATE).then_inc(attn_gate_ready, 1)
                        pe.wait_ge(y_done, attn + 1)
                        transposes(attn_a, y).then_inc(y_t_ready, 1)
                    if b == 5 and prep is not None:
                        router(n + 1, 1 - odd)
                    if b == 7 and attn is not None:
                        pe.wait_ge(attn_gate_done, attn + 1)
                        pe.wait_ge(y_norm_done, attn + 1)
                        transposes(attn_b, y_norm).then_inc(z_t_ready, 1)
                    if b == 8 and prep is not None:
                        gates_transpose(n + 1)
                    if b == 10 and attn is not None:
                        pe.wait_ge(z_lo_done, attn + 1)
                        product(attn_a[:], attn_w_hi[:, OUT, :], attn_w_lo[:, OUT, :], z_hi[:],
                                z_lo[:]).then_inc(attn_out_ready, 1)

            pe.wait_ge(ident_ready, 1)
            prep_transpose(0)
            pe.wait_ge(router_ready, 1)
            router(0, 0)
            pe.wait_ge(attn_loaded, 64)
            transposes(attn_a, attn_raw[:].rearrange("p k c -> p (k c)")).then_inc(attn_wt_ready, 1)
            gates_transpose(0)
            pe.wait_ge(expert_ready, 1)
            pe.wait_ge(attn_w_ready, 1)
            run_slots(pe, slot)
            for b in range(BLOCKS - DOWN_LAG, BLOCKS):
                down(BLOCKS * (UNITS - 1) + b, b, UNITS - 1)
            resid_transpose(UNITS - 1)


_INS = ["L0_attn_x", "L0_attn_Wq", "L0_attn_Wv", "L0_attn_Wg", "L0_attn_Wo", "L0_attn_beta", "L0_attn_ln_gamma",
        "L0_attn_ln_beta", "L0_ffn_w_gate", "L0_ffn_w_g", "L0_ffn_w_u", "L0_ffn_w_d"]


def kernel(**inputs):
    import numpy as _np
    import concourse.bacc as _bacc
    from concourse import mybir as _mybir
    from concourse.bass_utils import run_bass_kernel_spmd as _run

    nc = _bacc.Bacc("TRN2", target_bir_lowering=False, num_devices=1)
    arrays, args = {}, []
    for name in _INS:
        a = _np.ascontiguousarray(inputs[name])
        arrays[f"in_{name}_dram"] = a
        args.append(nc.dram_tensor(f"in_{name}_dram", a.shape, _mybir.dt.from_np(a.dtype), kind="ExternalInput").ap())
    shape = inputs["L0_attn_x"].shape
    args.append(nc.dram_tensor("out_dram", shape, _mybir.dt.float32, kind="ExternalOutput").ap())
    macaron_kernel(nc, *args)
    r = _run(nc, [arrays], core_ids=[0])
    return r.results[0]["out_dram"]
```

```python
from contextlib import ExitStack

import concourse.bass as bass
from concourse import mybir

F32 = mybir.dt.float32
F32R = mybir.dt.float32r
U32 = mybir.dt.uint32
ACT = mybir.ActivationFunctionType
ALU = mybir.AluOpType

P = 128
LN_EPS = 1e-5
EULER = 2.718281828459045
UNITS_AHEAD = 4
HI_LAG = 2
DOWN_LAG = 4
VALUE, QUERY, GATE, OUT = range(4)
SORTING = 6
WARM_UP_PRODUCTS = 24
WARM_UP = 3
FIRST_BLOCKS = 3
AT = dict(
    FIRST=dict(FIRST_TOP=0, UP_LO=2, FIRST_ROWS=0, FIRST_T_GATES=2, FIRST_GATES_COPY=2, DOWN_LO=3, DOWN_HI=1,
               GATE_LO=0, FIRST_ROUTER=0, ATTN_W=7),
    WITH=dict(SCALE_A=0, SCALE_P=3, SCALE_Y=5, EXP=7, Z=8, OUT_COPY=0, NORM_A=2, DOWN_COPY=4, HI_A=2, NORM_P=5,
              HI_P=6, SILU_A=5, NORM_Y=7, AFFINE=8, GATES_COPY=10, Z_HI=9, STATS_A=0, ADD_A=1, STATS_P=1,
              LO_A=2, ADD_UNIT=5, SCAN=3, STATS_Y=5, LO_P=6, TOP=7, GATE_ROWS=8, Z_LO=10, T_OUT=0, T_A=2,
              T_DOWN=4, VALUE_QUERY=3, T_P=5, GATE_Y=4, ROUTER=6, T_Z=7, T_GATES=9, OUTPUT=10),
    ALONE=dict(SCALE_P=3, EXP=7, OUT_COPY=0, DOWN_COPY=4, NORM_P=5, HI_P=6, GATES_COPY=10, ADD_A=1, STATS_P=2,
               ADD_UNIT=5, LO_P=6, TOP=7, GATE_ROWS=8, T_OUT=0, T_DOWN=4, T_P=5, ROUTER=6, T_GATES=9),
)


def macaron_kernel(nc, x_in, w_q, w_v, w_gate_attn, w_o, beta, ln_gamma, ln_beta, w_router, w_g, w_u, w_d, out):
    GROUPS, TOKENS, D = x_in.shape
    EXPERTS, _, HIDDEN = w_g.shape
    HEADS = beta.shape[0]
    TILES = TOKENS // P
    BLOCKS = EXPERTS * HIDDEN // P
    PER_EXPERT = P // EXPERTS
    UNITS = 2 * GROUPS
    HEAD_DIM = D // HEADS
    assert D == P and HIDDEN == PER_EXPERT * BLOCKS and TOKENS == 512

    def final_unit(g):
        return UNITS_AHEAD + 2 * g if g < GROUPS - UNITS_AHEAD else GROUPS + g

    def wait(eng, sem, count):
        if not isinstance(count, int) or count > 0:
            eng.wait_ge(sem, count)

    with ExitStack() as ctx:
        def sb(name, shape, dt=F32):
            return ctx.enter_context(nc.sbuf_tensor(name, shape, dt))

        def bank(name):
            return ctx.enter_context(nc.psum_tensor(name, [P, 512], F32))

        def sem(name):
            return ctx.enter_context(nc.semaphore(name))

        x = sb("x", [P, GROUPS * TOKENS])

        gate_raw = sb("gate_raw", [P, EXPERTS * HIDDEN])
        up_raw = sb("up_raw", [P, EXPERTS * HIDDEN])
        down_raw = sb("down_raw", [P, EXPERTS * HIDDEN])
        gate_hi, gate_lo, up_hi, up_lo, down_hi, down_lo = (
            sb(n, [P, BLOCKS, P], F32R) for n in ("gate_hi", "gate_lo", "up_hi", "up_lo", "down_hi", "down_lo"))
        router_raw = sb("router_raw", [P, EXPERTS])
        router_split = sb("router_split", [P, 2 * EXPERTS], F32R)
        attn_raw = sb("attn_raw", [P, 4, P])
        attn_w_hi = sb("attn_w_hi", [P, 4, P], F32R)
        attn_w_lo = sb("attn_w_lo", [P, 4, P], F32R)
        beta_col = sb("beta_col", [P, 1])
        decay = sb("decay", [P, 1])
        gamma_col = sb("gamma_col", [P, 1])
        shift_col = sb("shift_col", [P, 1])

        ident = sb("ident", [P, P])
        minus_half = sb("minus_half", [P, TILES])
        euler = sb("euler", [P, TILES])
        expert_id = sb("expert_id", [P, EXPERTS])

        act_pulse = sb("act_pulse", [P, 5])
        dve_pulse = sb("dve_pulse", [P, 7])

        xt_hi = [sb(f"xt_hi{i}", [P, TOKENS], F32R) for i in range(2)]
        xt_lo = [sb(f"xt_lo{i}", [P, TOKENS], F32R) for i in range(2)]
        gates = [sb(f"gates{i}", [P, TOKENS]) for i in range(2)]
        silu = sb("silu", [P, 2, TOKENS])
        hidden = sb("hidden", [P, BLOCKS, TOKENS])
        hidden_hi = sb("hidden_hi", [P, BLOCKS, TOKENS], F32R)
        hidden_lo = sb("hidden_lo", [P, BLOCKS, TOKENS], F32R)
        half_down = sb("half_down", [P, TOKENS])

        prep_xn = sb("prep_xn", [P, TOKENS])
        prep_bn = sb("prep_bn", [P, TILES, 6])
        prep_mv = sb("prep_mv", [P, TILES, 2])
        prep_ve = sb("prep_ve", [P, TILES])
        prep_nm = sb("prep_nm", [P, TILES])
        prep_rstd = sb("prep_rstd", [P, TILES])
        prep_bias = sb("prep_bias", [P, TILES])
        scores = sb("scores", [P, TILES, EXPERTS])
        scores_half = sb("scores_half", [P, TILES, EXPERTS])
        sorted_scores = sb("sorted_scores", [P, TILES, 8])
        sorted_ids = sb("sorted_ids", [P, TILES, 8], U32)
        top_ids = sb("top_ids", [P, TILES, 2])
        is_top = sb("is_top", [P, TILES, 2, EXPERTS])
        top_gap = sb("top_gap", [P, TILES])
        top_exp = sb("top_exp", [P, TILES])
        top_sum = sb("top_sum", [P, TILES])
        top_prob = sb("top_prob", [P, TILES, 2])
        top_gate = sb("top_gate", [P, TILES, 2, EXPERTS])
        gates_tok = sb("gates_tok", [P, TILES, EXPERTS, PER_EXPERT])

        attn_xn = sb("attn_xn", [P, TOKENS])
        attn_bn = sb("attn_bn", [P, TILES, 6])
        attn_mv = sb("attn_mv", [P, TILES, 2])
        attn_ve = sb("attn_ve", [P, TILES])
        attn_nm = sb("attn_nm", [P, TILES])
        attn_rstd = sb("attn_rstd", [P, TILES])
        attn_bias = sb("attn_bias", [P, TILES])
        attn_xt_hi = sb("attn_xt_hi", [P, TOKENS], F32R)
        attn_xt_lo = sb("attn_xt_lo", [P, TOKENS], F32R)
        state = sb("state", [P, TOKENS])
        y = sb("y", [P, TOKENS])
        y_bn = sb("y_bn", [P, TILES, 6])
        y_mv = sb("y_mv", [P, TILES, 2])
        y_ve = sb("y_ve", [P, TILES])
        y_nm = sb("y_nm", [P, TILES])
        y_rstd = sb("y_rstd", [P, TILES])
        y_bias = sb("y_bias", [P, TILES])
        y_norm = sb("y_norm", [P, TOKENS])
        attn_gate = sb("attn_gate", [P, TOKENS])
        z_affine = sb("z_affine", [P, TOKENS])
        z = sb("z", [P, TOKENS])
        z_hi = sb("z_hi", [P, TOKENS], F32R)
        z_lo = sb("z_lo", [P, TOKENS], F32R)
        attn_out = sb("attn_out", [P, TOKENS])

        gate_ps = [bank(f"gate_ps{i}") for i in range(2)]
        up_ps = [bank(f"up_ps{i}") for i in range(2)]
        down_ps = bank("down_ps")
        prep_ps = bank("prep_ps")
        attn_a = bank("attn_a")
        attn_b = bank("attn_b")

        x0_loaded = sem("x0_loaded")
        x_loaded = sem("x_loaded")
        router_loaded = sem("router_loaded")
        gate_loaded = sem("gate_loaded")
        up_loaded = sem("up_loaded")
        down_loaded = sem("down_loaded")
        attn_loaded = sem("attn_loaded")
        beta_loaded = sem("beta_loaded")
        columns_loaded = sem("columns_loaded")
        ident_zero = sem("ident_zero")
        ident_ready = sem("ident_ready")
        consts_ready = sem("consts_ready")
        router_hi_ready = sem("router_hi_ready")
        router_ready = sem("router_ready")
        expert_hi_ready = sem("expert_hi_ready")
        expert_ready = sem("expert_ready")
        decay_ready = sem("decay_ready")
        attn_wt_ready = sem("attn_wt_ready")
        attn_w_hi_ready = sem("attn_w_hi_ready")
        attn_w_ready = sem("attn_w_ready")
        gate_ready = sem("gate_ready")
        up_ready = sem("up_ready")
        silu_done = sem("silu_done")
        product_done = sem("product_done")
        gated_done = sem("gated_done")
        hidden_hi_done = sem("hidden_hi_done")
        hidden_lo_done = sem("hidden_lo_done")
        down_done = sem("down_done")
        down_copied = sem("down_copied")
        resid_t_ready = sem("resid_t_ready")
        resid_done = sem("resid_done")
        prep_bn_done = sem("prep_bn_done")
        prep_mv_done = sem("prep_mv_done")
        prep_stats_done = sem("prep_stats_done")
        prep_rstd_done = sem("prep_rstd_done")
        prep_scale_done = sem("prep_scale_done")
        prep_norm_done = sem("prep_norm_done")
        prep_t_ready = sem("prep_t_ready")
        prep_hi_done = sem("prep_hi_done")
        prep_lo_done = sem("prep_lo_done")
        scores_ready = sem("scores_ready")
        scores_half_copied = sem("scores_half_copied")
        scores_copied = sem("scores_copied")
        sorted_done = sem("sorted_done")
        ids_done = sem("ids_done")
        gap_done = sem("gap_done")
        exp_done = sem("exp_done")
        top_ids_done = sem("top_ids_done")
        is_top_done = sem("is_top_done")
        sum_done = sem("sum_done")
        first_prob_done = sem("first_prob_done")
        probs_done = sem("probs_done")
        top_gate_done = sem("top_gate_done")
        gates_tok_done = sem("gates_tok_done")
        gates_t_ready = sem("gates_t_ready")
        gates_done = sem("gates_done")
        attn_bn_done = sem("attn_bn_done")
        attn_mv_done = sem("attn_mv_done")
        attn_stats_done = sem("attn_stats_done")
        attn_rstd_done = sem("attn_rstd_done")
        attn_scale_done = sem("attn_scale_done")
        attn_norm_done = sem("attn_norm_done")
        attn_t_ready = sem("attn_t_ready")
        attn_hi_done = sem("attn_hi_done")
        attn_lo_done = sem("attn_lo_done")
        value_ready = sem("value_ready")
        query_ready = sem("query_ready")
        attn_gate_ready = sem("attn_gate_ready")
        state_done = sem("state_done")
        attn_gate_done = sem("attn_gate_done")
        y_done = sem("y_done")
        y_t_ready = sem("y_t_ready")
        y_bn_done = sem("y_bn_done")
        y_mv_done = sem("y_mv_done")
        y_stats_done = sem("y_stats_done")
        y_rstd_done = sem("y_rstd_done")
        y_scale_done = sem("y_scale_done")
        y_norm_done = sem("y_norm_done")
        z_t_ready = sem("z_t_ready")
        z_affine_done = sem("z_affine_done")
        z_done = sem("z_done")
        z_hi_done = sem("z_hi_done")
        z_lo_done = sem("z_lo_done")
        attn_out_ready = sem("attn_out_ready")
        attn_out_copied = sem("attn_out_copied")
        attn_resid_t_ready = sem("attn_resid_t_ready")
        attn_resid_done = sem("attn_resid_done")
        stored = sem("stored")

        def run_slots(eng, slot):
            slot(n=0, odd=0, prep=1)
            slot(n=1, odd=1, prep=2, done=0)
            with eng.Fori(0, 4) as i:
                first = 1 // (i + 1)
                even_done = nc.s_assert_within((i + 2) - first, 1, 5, skip_runtime_bounds_check_because="i is in 0..3")
                odd_done = nc.s_assert_within((i + 3 * first) - 1, 0, 2, skip_runtime_bounds_check_because="i is in 0..3")
                slot(n=2 * i + 2, odd=0, prep=i + 3, attn=i, done=even_done)
                slot(n=2 * i + 3, odd=1, prep=i, left=i, done=odd_done)
            slot(n=10, odd=0, prep=7, attn=4, done=6)
            slot(n=11, odd=1, prep=4, attn=5, left=4, done=3)
            slot(n=12, odd=0, prep=5, attn=6, left=5, done=7)
            slot(n=13, odd=1, prep=6, attn=7, left=6, done=4)
            slot(n=14, odd=0, prep=7, left=7, done=5)
            slot(n=15, odd=1, done=6)

        gate_source = gate_raw[:].rearrange("k (p b) -> k b p", b=BLOCKS)
        up_source = up_raw[:].rearrange("k (p b) -> k b p", b=BLOCKS)
        down_source = down_raw[:].rearrange("k (b d) -> k b d", b=BLOCKS)

        block = ctx.enter_context(nc.Block())

        @block.sync
        def _(sp):
            xv = x[:].rearrange("p (g t d) -> p g t d", t=TILES, d=D)
            sp.dma_start(xv[:, 0], x_in[0].rearrange("(t p) d -> p t d", p=P)).then_inc(x0_loaded, 16)
            sp.dma_start(gate_raw[:].rearrange("d (e m) -> d e m", e=EXPERTS),
                         w_g.rearrange("e d m -> d e m")).then_inc(gate_loaded, 16)
            sp.dma_start(up_raw[:].rearrange("d (e m) -> d e m", e=EXPERTS),
                         w_u.rearrange("e d m -> d e m")).then_inc(up_loaded, 16)
            sp.dma_start(down_raw[:], w_d.rearrange("e m d -> (e m) d").rearrange(
                "(p b) d -> p (b d)", b=BLOCKS)).then_inc(down_loaded, 16)
            for g in range(1, GROUPS):
                sp.dma_start(xv[:, g], x_in[g].rearrange("(t p) d -> p t d", p=P)).then_inc(x_loaded, 16)
            for k, w in ((VALUE, w_v), (QUERY, w_q), (GATE, w_gate_attn), (OUT, w_o)):
                sp.dma_start(attn_raw[:, k, :], w).then_inc(attn_loaded, 16)
            sp.dma_start(gamma_col[:], ln_gamma.rearrange("(d o) -> d o", o=1)).then_inc(columns_loaded, 16)
            sp.dma_start(shift_col[:], ln_beta.rearrange("(d o) -> d o", o=1)).then_inc(columns_loaded, 16)
            for g in range(GROUPS):
                sp.wait_ge(resid_done, final_unit(g) + 1)
                sp.dma_start(out[g].rearrange("(t p) d -> p t d", p=P), xv[:, g]).then_inc(stored, 16)
            sp.wait_ge(stored, 16 * GROUPS)

        @block.gpsimd
        def _(pool):
            nc.gpsimd.memset(ident[:], 0.0).then_inc(ident_zero, 1)
            pool.wait_ge(ident_zero, 1)
            nc.gpsimd.affine_select(out=ident[:], in_=ident[:], compare_op=ALU.not_equal, fill=1.0, base=0,
                                    pattern=[[-1, P]], channel_multiplier=1).then_inc(ident_ready, 1)
            nc.gpsimd.memset(minus_half[:], -0.5)
            nc.gpsimd.memset(euler[:], EULER)
            for e in range(EXPERTS):
                last = nc.gpsimd.memset(expert_id[:, e:e + 1], float(e))
            last.then_inc(consts_ready, 1)
            pool.wait_ge(consts_ready, 1)

            def scale_of(ve, nm, rstd, bias, stats_done, rstd_done, scale_done, count):
                pool.wait_ge(stats_done, count)
                nc.gpsimd.tensor_tensor(rstd[:], ve[:], minus_half[:], ALU.pow).then_inc(rstd_done, 1)
                pool.wait_ge(rstd_done, count)
                nc.gpsimd.tensor_tensor(bias[:], nm[:], rstd[:], ALU.mult).then_inc(scale_done, 1)

            def prep_scale(p):
                scale_of(prep_ve, prep_nm, prep_rstd, prep_bias, prep_stats_done, prep_rstd_done, prep_scale_done, p + 1)

            def top_exponential(p):
                pool.wait_ge(gap_done, p + 1)
                nc.gpsimd.tensor_tensor(top_exp[:], euler[:], top_gap[:], ALU.pow).then_inc(exp_done, 1)

            def slot(n, odd, prep=None, attn=None, left=None, done=None):
                at = AT["ALONE" if attn is None else "WITH"]
                for b in range(BLOCKS):
                    if attn is not None and b == at["SCALE_A"]:
                        scale_of(attn_ve, attn_nm, attn_rstd, attn_bias, attn_stats_done, attn_rstd_done,
                                 attn_scale_done, attn + 1)
                    if b == at["SCALE_P"] and prep is not None:
                        prep_scale(n + 1)
                    if attn is not None and b == at["SCALE_Y"]:
                        scale_of(y_ve, y_nm, y_rstd, y_bias, y_stats_done, y_rstd_done, y_scale_done, attn + 1)
                    if b == at["EXP"] and prep is not None:
                        top_exponential(n + 1)
                    if attn is not None and b == at["Z"]:
                        pool.wait_ge(z_affine_done, attn + 1)
                        pool.wait_ge(attn_gate_done, attn + 1)
                        nc.gpsimd.tensor_tensor(z[:], z_affine[:], attn_gate[:], ALU.mult).then_inc(z_done, 1)
                    if b == 0:
                        pool.wait_ge(gates_done, n + 1)
                    pool.wait_ge(product_done, BLOCKS * n + b + 1)
                    nc.gpsimd.tensor_tensor(hidden[:, b, :], hidden[:, b, :], gates[odd][:],
                                            ALU.mult).then_inc(gated_done, 1)

            prep_scale(0)
            top_exponential(0)
            run_slots(pool, slot)

        @block.scalar
        def _(act):
            act.dma_start(beta_col[:], beta.rearrange("(h o) -> h o", o=1).broadcast_to(
                [HEADS, HEAD_DIM])).then_inc(beta_loaded, 16)
            act.dma_start(router_raw[:], w_router).then_inc(router_loaded, 16)
            act.wait_ge(consts_ready, 1)
            nc.scalar.activation(act_pulse[:, WARM_UP:WARM_UP + 1], minus_half[:, 0:1], ACT.Sigmoid)
            act.wait_ge(beta_loaded, 16)
            nc.scalar.activation(decay[:], beta_col[:], ACT.Sigmoid).then_inc(decay_ready, 1)
            nc.scalar.activation(act_pulse[:, WARM_UP + 1:WARM_UP + 2], minus_half[:, 0:1], ACT.Silu)

            def normalise(dst, src_tile, rstd, bias, scale_done, norm_done, count, pulse):
                act.wait_ge(scale_done, count)
                nc.scalar.activation(act_pulse[:, pulse:pulse + 1], minus_half[:, 0:1], ACT.Copy)
                for t in range(TILES):
                    last = nc.scalar.activation(dst[:, t * P:(t + 1) * P], src_tile(t), ACT.Identity,
                                                bias=bias[:, t:t + 1], scale=rstd[:, t:t + 1])
                last.then_inc(norm_done, 1)

            def prep_norm(p, g):
                wait(act, prep_t_ready, p)
                normalise(prep_xn, lambda t: x[:, bass.ds(g * TOKENS + t * P, P)], prep_rstd, prep_bias,
                          prep_scale_done, prep_norm_done, p + 1, pulse=0)

            def prep_hi(p, odd):
                act.wait_ge(prep_t_ready, p + 1)
                nc.scalar.activation(xt_hi[odd][:], prep_ps[:], ACT.Copy).then_inc(prep_hi_done, 1)

            def gates_copy(p, odd):
                act.wait_ge(gates_t_ready, p + 1)
                nc.scalar.activation(gates[odd][:], prep_ps[:], ACT.Copy).then_inc(gates_done, 1)

            def weight_hi(hi, source, blocks):
                nc.scalar.activation(hi[:, blocks, :], source[:, blocks, :], ACT.Copy).then_inc(expert_hi_ready, 1)

            def hidden_split(q, b):
                act.wait_ge(gated_done, q + 1)
                wait(act, down_done, q + 1 - BLOCKS)
                nc.scalar.activation(hidden_hi[:, b, :], hidden[:, b, :], ACT.Copy).then_inc(hidden_hi_done, 1)

            def copy_down(n):
                act.wait_ge(down_done, BLOCKS * (n + 1))
                wait(act, resid_t_ready, n)
                nc.scalar.activation(half_down[:], down_ps[:], ACT.Copy, scale=0.5).then_inc(down_copied, 1)

            def slot(n, odd, prep=None, attn=None, left=None, done=None):
                at = AT["ALONE" if attn is None else "WITH"]
                for b in range(BLOCKS):
                    if b == at["OUT_COPY"] and left is not None:
                        act.wait_ge(attn_out_ready, left + 1)
                        nc.scalar.activation(attn_out[:], attn_a[:], ACT.Copy).then_inc(attn_out_copied, 1)
                    if attn is not None and b == at["NORM_A"]:
                        wait(act, attn_t_ready, attn)
                        normalise(attn_xn, lambda t: x[:, bass.ds(attn * TOKENS + t * P, P)], attn_rstd, attn_bias,
                                  attn_scale_done, attn_norm_done, attn + 1, pulse=1)
                    if b == at["DOWN_COPY"] and done is not None:
                        copy_down(n - 1)
                    if attn is not None and b == at["HI_A"]:
                        act.wait_ge(attn_t_ready, attn + 1)
                        nc.scalar.activation(attn_xt_hi[:], attn_a[:], ACT.Copy).then_inc(attn_hi_done, 1)
                    if b == at["NORM_P"] and prep is not None:
                        prep_norm(n + 1, prep)
                    if b == at["HI_P"] and prep is not None:
                        prep_hi(n + 1, 1 - odd)
                    if attn is not None and b == at["SILU_A"]:
                        act.wait_ge(attn_gate_ready, attn + 1)
                        nc.scalar.activation(attn_gate[:], attn_b[:], ACT.Silu).then_inc(attn_gate_done, 1)
                    if attn is not None and b == at["NORM_Y"]:
                        normalise(y_norm, lambda t: attn_a[:, t * P:(t + 1) * P], y_rstd, y_bias,
                                  y_scale_done, y_norm_done, attn + 1, pulse=2)
                    if attn is not None and b == at["AFFINE"]:
                        act.wait_ge(z_t_ready, attn + 1)
                        nc.scalar.activation(z_affine[:], attn_b[:], ACT.Identity, bias=shift_col[:, 0:1],
                                             scale=gamma_col[:, 0:1]).then_inc(z_affine_done, 1)
                    if b == at["GATES_COPY"] and prep is not None:
                        gates_copy(n + 1, 1 - odd)
                    if attn is not None and b == at["Z_HI"]:
                        act.wait_ge(z_done, attn + 1)
                        nc.scalar.activation(z_hi[:], z[:], ACT.Copy).then_inc(z_hi_done, 1)
                    if isinstance(n, int) and n == 0 and b == AT["FIRST"]["DOWN_HI"]:
                        act.wait_ge(down_loaded, 16)
                        weight_hi(down_hi, down_source, slice(0, BLOCKS))
                    if isinstance(n, int) and n == 0 and b == AT["FIRST"]["FIRST_GATES_COPY"]:
                        gates_copy(0, 0)
                    if isinstance(n, int) and n == 0 and b == AT["FIRST"]["ATTN_W"]:
                        act.wait_ge(columns_loaded, 32)
                        act.wait_ge(attn_wt_ready, 1)
                        nc.scalar.activation(attn_w_hi[:].rearrange("p k c -> p (k c)"), attn_a[:],
                                             ACT.Copy).then_inc(attn_w_hi_ready, 1)
                    q = BLOCKS * n + b
                    act.wait_ge(gate_ready, q + 1)
                    wait(act, product_done, q - 1)
                    nc.scalar.activation(silu[:, (odd + b) % 2, :], gate_ps[(odd + b) % 2][:],
                                         ACT.Silu).then_inc(silu_done, 1)
                    if not isinstance(n, int) or n > 0 or b >= HI_LAG:
                        hidden_split(q - HI_LAG, (b - HI_LAG) % BLOCKS)

            act.wait_ge(router_loaded, 16)
            nc.scalar.activation(router_split[:, 0:EXPERTS], router_raw[:], ACT.Copy).then_inc(router_hi_ready, 1)
            act.wait_ge(x0_loaded, 16)
            prep_norm(0, 0)
            first, rest = slice(0, FIRST_BLOCKS), slice(FIRST_BLOCKS, BLOCKS)
            act.wait_ge(gate_loaded, 16)
            weight_hi(gate_hi, gate_source, first)
            act.wait_ge(up_loaded, 16)
            weight_hi(up_hi, up_source, first)
            prep_hi(0, 0)
            weight_hi(gate_hi, gate_source, rest)
            weight_hi(up_hi, up_source, rest)
            run_slots(act, slot)
            for b in range(BLOCKS - HI_LAG, BLOCKS):
                hidden_split(BLOCKS * (UNITS - 1) + b, b)
            copy_down(UNITS - 1)

        @block.vector
        def _(dve):
            def stand_in(pulse):
                nc.vector.memset(dve_pulse[:, pulse:pulse + 1], 0.0)

            def moments(src_tile, bn, mv, ve, nm, bn_done, mv_done, stats_done, count, pulse):
                stand_in(pulse + 1)
                for t in range(TILES):
                    last = nc.vector.bn_stats(bn[:, t, :], src_tile(t))
                last.then_inc(bn_done, 1)
                dve.wait_ge(bn_done, count)
                stand_in(pulse)
                for t in range(TILES):
                    last = nc.vector.bn_aggr(mv[:, t, :], bn[:, t, :])
                last.then_inc(mv_done, 1)
                dve.wait_ge(mv_done, count)
                nc.vector.tensor_scalar(ve[:], mv[:, :, 1], LN_EPS, None, ALU.add)
                nc.vector.tensor_scalar(nm[:], mv[:, :, 0], -1.0, None, ALU.mult).then_inc(stats_done, 1)

            def prep_moments(p, g):
                moments(lambda t: x[:, bass.ds(g * TOKENS + t * P, P)], prep_bn, prep_mv, prep_ve, prep_nm,
                        prep_bn_done, prep_mv_done, prep_stats_done, p + 1, pulse=0)

            def prep_lo(p, odd):
                dve.wait_ge(prep_hi_done, p + 1)
                nc.vector.tensor_tensor(xt_lo[odd][:], prep_ps[:], xt_hi[odd][:].bitcast(F32),
                                        ALU.subtract).then_inc(prep_lo_done, 1)

            def top_two(p):
                dve.wait_ge(scores_ready, p + 1)
                halves = prep_ps[:, 0:2 * TILES * EXPERTS].rearrange("p (t h e) -> p t h e", h=2, e=EXPERTS)
                nc.vector.tensor_copy(scores_half[:], halves[:, :, 1, :]).then_inc(scores_half_copied, 1)
                dve.wait_ge(scores_half_copied, p + 1)
                nc.vector.tensor_tensor(scores[:], halves[:, :, 0, :], scores_half[:], ALU.add).then_inc(scores_copied, 1)
                dve.wait_ge(scores_copied, p + 1)
                stand_in(SORTING)
                for t in range(TILES):
                    last = nc.vector.max(sorted_scores[:, t, :], scores[:, t, :])
                last.then_inc(sorted_done, 1)
                dve.wait_ge(sorted_done, p + 1)
                nc.vector.tensor_tensor(top_gap[:], sorted_scores[:, :, 1], sorted_scores[:, :, 0],
                                        ALU.subtract).then_inc(gap_done, 1)
                for t in range(TILES):
                    last = nc.vector.max_index(sorted_ids[:, t, :], sorted_scores[:, t, :], scores[:, t, :])
                last.then_inc(ids_done, 1)
                dve.wait_ge(ids_done, p + 1)
                nc.vector.tensor_copy(top_ids[:], sorted_ids[:, :, 0:2]).then_inc(top_ids_done, 1)
                dve.wait_ge(top_ids_done, p + 1)
                shape = [P, TILES, 2, EXPERTS]
                nc.vector.tensor_tensor(is_top[:], expert_id[:].unsqueeze(1).unsqueeze(1).broadcast_to(shape),
                                        top_ids[:].unsqueeze(3).broadcast_to(shape),
                                        ALU.is_equal).then_inc(is_top_done, 1)

            def gate_rows(p):
                dve.wait_ge(exp_done, p + 1)
                nc.vector.tensor_scalar(top_sum[:], top_exp[:], 1.0, None, ALU.add).then_inc(sum_done, 1)
                dve.wait_ge(sum_done, p + 1)
                nc.vector.reciprocal(top_prob[:, :, 0], top_sum[:]).then_inc(first_prob_done, 1)
                dve.wait_ge(first_prob_done, p + 1)
                nc.vector.tensor_tensor(top_prob[:, :, 1], top_prob[:, :, 0], top_exp[:],
                                        ALU.mult).then_inc(probs_done, 1)
                dve.wait_ge(probs_done, p + 1)
                dve.wait_ge(is_top_done, p + 1)
                nc.vector.tensor_tensor(top_gate[:], is_top[:],
                                        top_prob[:].unsqueeze(3).broadcast_to([P, TILES, 2, EXPERTS]),
                                        ALU.mult).then_inc(top_gate_done, 1)
                dve.wait_ge(top_gate_done, p + 1)
                shape = [P, TILES, EXPERTS, PER_EXPERT]
                nc.vector.tensor_tensor(gates_tok[:], top_gate[:, :, 0, :].unsqueeze(3).broadcast_to(shape),
                                        top_gate[:, :, 1, :].unsqueeze(3).broadcast_to(shape),
                                        ALU.add).then_inc(gates_tok_done, 1)

            def weight_lo(count, hi, lo, source, blocks):
                dve.wait_ge(expert_hi_ready, count)
                nc.vector.tensor_tensor(lo[:, blocks, :], source[:, blocks, :], hi[:, blocks, :].bitcast(F32),
                                        ALU.subtract).then_inc(expert_ready, 1)

            def hidden_rest(q, b):
                dve.wait_ge(hidden_hi_done, q + 1)
                nc.vector.tensor_tensor(hidden_lo[:, b, :], hidden[:, b, :], hidden_hi[:, b, :].bitcast(F32),
                                        ALU.subtract).then_inc(hidden_lo_done, 1)

            def add_unit(n, g):
                dve.wait_ge(resid_t_ready, n + 1)
                xg = x[:, bass.ds(g * TOKENS, TOKENS)]
                nc.vector.tensor_tensor(xg, prep_ps[:], xg, ALU.add).then_inc(resid_done, 1)

            def slot(n, odd, prep=None, attn=None, left=None, done=None):
                at = AT["ALONE" if attn is None else "WITH"]
                for b in range(BLOCKS):
                    if attn is not None and b == at["STATS_A"]:
                        dve.wait_ge(resid_done, n - 1)
                        moments(lambda t: x[:, bass.ds(attn * TOKENS + t * P, P)], attn_bn, attn_mv, attn_ve, attn_nm,
                                attn_bn_done, attn_mv_done, attn_stats_done, attn + 1, pulse=2)
                    if b == at["ADD_A"] and left is not None:
                        dve.wait_ge(attn_resid_t_ready, left + 1)
                        xg = x[:, bass.ds(left * TOKENS, TOKENS)]
                        nc.vector.tensor_tensor(xg, attn_b[:], xg, ALU.add).then_inc(attn_resid_done, 1)
                    if b == at["STATS_P"] and prep is not None:
                        if isinstance(n, int) and n == 0:
                            dve.wait_ge(x_loaded, 16 * (GROUPS - 1))
                        if left is not None:
                            dve.wait_ge(attn_resid_done, left + 1)
                        prep_moments(n + 1, prep)
                    if attn is not None and b == at["LO_A"]:
                        dve.wait_ge(attn_hi_done, attn + 1)
                        nc.vector.tensor_tensor(attn_xt_lo[:], attn_a[:], attn_xt_hi[:].bitcast(F32),
                                                ALU.subtract).then_inc(attn_lo_done, 1)
                    if b == at["ADD_UNIT"] and done is not None:
                        add_unit(n - 1, done)
                    if attn is not None and b == at["SCAN"]:
                        dve.wait_ge(value_ready, attn + 1)
                        nc.vector.tensor_tensor_scan(state[:], decay[:, 0:1].to_broadcast([P, TOKENS]), attn_b[:],
                                                     0.0, ALU.mult, ALU.add).then_inc(state_done, 1)
                        dve.wait_ge(state_done, attn + 1)
                        dve.wait_ge(query_ready, attn + 1)
                        nc.vector.tensor_tensor(y[:], attn_a[:], state[:], ALU.mult).then_inc(y_done, 1)
                    if attn is not None and b == at["STATS_Y"]:
                        dve.wait_ge(y_t_ready, attn + 1)
                        moments(lambda t: attn_a[:, t * P:(t + 1) * P], y_bn, y_mv, y_ve, y_nm,
                                y_bn_done, y_mv_done, y_stats_done, attn + 1, pulse=4)
                    if b == at["LO_P"] and prep is not None:
                        prep_lo(n + 1, 1 - odd)
                    if b == at["TOP"] and prep is not None:
                        top_two(n + 1)
                    if b == at["GATE_ROWS"] and prep is not None:
                        gate_rows(n + 1)
                    if attn is not None and b == at["Z_LO"]:
                        dve.wait_ge(z_hi_done, attn + 1)
                        nc.vector.tensor_tensor(z_lo[:], z[:], z_hi[:].bitcast(F32),
                                                ALU.subtract).then_inc(z_lo_done, 1)
                    if isinstance(n, int) and n == 0:
                        if b == AT["FIRST"]["FIRST_TOP"]:
                            top_two(0)
                        if b == AT["FIRST"]["GATE_LO"]:
                            weight_lo(3, gate_hi, gate_lo, gate_source, slice(FIRST_BLOCKS, BLOCKS))
                        if b == AT["FIRST"]["UP_LO"]:
                            weight_lo(4, up_hi, up_lo, up_source, slice(FIRST_BLOCKS, BLOCKS))
                        if b == AT["FIRST"]["FIRST_ROWS"]:
                            gate_rows(0)
                        if b == AT["FIRST"]["DOWN_LO"]:
                            weight_lo(5, down_hi, down_lo, down_source, slice(0, BLOCKS))
                        if b == AT["FIRST"]["ATTN_W"]:
                            dve.wait_ge(attn_w_hi_ready, 1)
                            nc.vector.tensor_tensor(attn_w_lo[:].rearrange("p k c -> p (k c)"), attn_a[:],
                                                    attn_w_hi[:].rearrange("p k c -> p (k c)").bitcast(F32),
                                                    ALU.subtract).then_inc(attn_w_ready, 1)
                    q = BLOCKS * n + b
                    dve.wait_ge(silu_done, q + 1)
                    dve.wait_ge(up_ready, q + 1)
                    nc.vector.tensor_tensor(hidden[:, b, :], up_ps[(odd + b) % 2][:], silu[:, (odd + b) % 2, :],
                                            ALU.mult).then_inc(product_done, 1)
                    if not isinstance(n, int) or n > 0 or b >= HI_LAG:
                        hidden_rest(q - HI_LAG, (b - HI_LAG) % BLOCKS)

            dve.wait_ge(x0_loaded, 16)
            prep_moments(0, 0)
            dve.wait_ge(router_hi_ready, 1)
            nc.vector.tensor_tensor(router_split[:, EXPERTS:2 * EXPERTS], router_raw[:],
                                    router_split[:, 0:EXPERTS].bitcast(F32), ALU.subtract).then_inc(router_ready, 1)
            first = slice(0, FIRST_BLOCKS)
            weight_lo(1, gate_hi, gate_lo, gate_source, first)
            weight_lo(2, up_hi, up_lo, up_source, first)
            prep_lo(0, 0)
            dve.wait_ge(consts_ready, 1)
            dve.wait_ge(decay_ready, 1)
            run_slots(dve, slot)
            for b in range(BLOCKS - HI_LAG, BLOCKS):
                hidden_rest(BLOCKS * (UNITS - 1) + b, b)
            add_unit(UNITS - 1, GROUPS - 1)

        @block.tensor
        def _(pe):
            def product(dst, w_hi, w_lo, v_hi, v_lo, start=True, stop=True):
                nc.tensor.matmul(dst, w_hi, v_hi, start=start, stop=False)
                nc.tensor.matmul(dst, w_hi, v_lo, start=False, stop=False)
                return nc.tensor.matmul(dst, w_lo, v_hi, start=False, stop=stop)

            def transposes(dst, src):
                for t in range(TILES):
                    last = nc.tensor.transpose(dst[:, t * P:(t + 1) * P], src[:, t * P:(t + 1) * P], ident[:])
                return last

            def prep_transpose(p):
                wait(pe, gates_done, p)
                wait(pe, resid_done, p - 1)
                pe.wait_ge(prep_norm_done, p + 1)
                transposes(prep_ps, prep_xn).then_inc(prep_t_ready, 1)

            def router(p, odd):
                pe.wait_ge(prep_lo_done, p + 1)
                for t in range(TILES):
                    cols = slice(t * P, (t + 1) * P)
                    dst = prep_ps[:, 2 * t * EXPERTS:2 * (t + 1) * EXPERTS]
                    nc.tensor.matmul(dst, xt_hi[odd][:, cols], router_split[:], start=True, stop=False)
                    last = nc.tensor.matmul(dst, xt_lo[odd][:, cols], router_split[:], start=False, stop=True)
                last.then_inc(scores_ready, 1)

            def gates_transpose(p):
                pe.wait_ge(scores_copied, p + 1)
                pe.wait_ge(gates_tok_done, p + 1)
                transposes(prep_ps, gates_tok[:].rearrange("p t e r -> p (t e r)")).then_inc(gates_t_ready, 1)

            def down(q, b, n):
                pe.wait_ge(hidden_lo_done, q + 1)
                if b == 0:
                    wait(pe, down_copied, n)
                product(down_ps[:], down_hi[:, b, :], down_lo[:, b, :], hidden_hi[:, b, :], hidden_lo[:, b, :],
                        start=b == 0, stop=b == BLOCKS - 1).then_inc(down_done, 1)

            def attn_product(dst, k):
                return product(dst[:], attn_w_hi[:, k, :], attn_w_lo[:, k, :], attn_xt_hi[:], attn_xt_lo[:])

            def resid_transpose(n):
                wait(pe, gates_done, n + 2 if not isinstance(n, int) or n + 1 < UNITS else UNITS)
                pe.wait_ge(down_copied, n + 1)
                transposes(prep_ps, half_down).then_inc(resid_t_ready, 1)

            def slot(n, odd, prep=None, attn=None, left=None, done=None):
                at = AT["ALONE" if attn is None else "WITH"]
                pe.wait_ge(prep_lo_done, n + 1)
                for b in range(BLOCKS):
                    q = BLOCKS * n + b
                    if isinstance(n, int) and n == 0:
                        if b == 0:
                            pe.wait_ge(expert_ready, 1)
                        if b == FIRST_BLOCKS:
                            pe.wait_ge(expert_ready, 3)
                        if b == AT["FIRST"]["FIRST_ROUTER"]:
                            pe.wait_ge(router_ready, 1)
                            router(0, 0)
                        if b == AT["FIRST"]["FIRST_T_GATES"]:
                            gates_transpose(0)
                        if b == AT["FIRST"]["ATTN_W"]:
                            pe.wait_ge(attn_loaded, 64)
                            transposes(attn_a, attn_raw[:].rearrange("p k c -> p (k c)")).then_inc(attn_wt_ready, 1)
                    wait(pe, silu_done, q - 1)
                    product(gate_ps[(odd + b) % 2][:], gate_hi[:, b, :], gate_lo[:, b, :],
                            xt_hi[odd][:], xt_lo[odd][:]).then_inc(gate_ready, 1)
                    if isinstance(n, int) and n == 0 and b == 0:
                        pe.wait_ge(expert_ready, 2)
                    if isinstance(n, int) and n == 0 and b == FIRST_BLOCKS:
                        pe.wait_ge(expert_ready, 4)
                    wait(pe, product_done, q - 1)
                    product(up_ps[(odd + b) % 2][:], up_hi[:, b, :], up_lo[:, b, :],
                            xt_hi[odd][:], xt_lo[odd][:]).then_inc(up_ready, 1)
                    if isinstance(n, int) and n == 0 and b == DOWN_LAG:
                        pe.wait_ge(expert_ready, 5)
                    if isinstance(n, int) and n == 1 and b == 0:
                        pe.wait_ge(attn_w_ready, 1)
                    if not isinstance(n, int) or n > 0 or b >= DOWN_LAG:
                        down(q - DOWN_LAG, (b - DOWN_LAG) % BLOCKS, n)
                    if b == at["T_OUT"] and left is not None:
                        pe.wait_ge(attn_out_copied, left + 1)
                        transposes(attn_b, attn_out).then_inc(attn_resid_t_ready, 1)
                    if attn is not None and b == at["T_A"]:
                        wait(pe, attn_out_copied, attn)
                        pe.wait_ge(attn_norm_done, attn + 1)
                        transposes(attn_a, attn_xn).then_inc(attn_t_ready, 1)
                    if b == at["T_DOWN"] and done is not None:
                        resid_transpose(n - 1)
                    if attn is not None and b == at["VALUE_QUERY"]:
                        wait(pe, attn_resid_done, attn)
                        pe.wait_ge(attn_lo_done, attn + 1)
                        attn_product(attn_b, VALUE).then_inc(value_ready, 1)
                        attn_product(attn_a, QUERY).then_inc(query_ready, 1)
                    if b == at["T_P"] and prep is not None:
                        prep_transpose(n + 1)
                    if attn is not None and b == at["GATE_Y"]:
                        pe.wait_ge(state_done, attn + 1)
                        attn_product(attn_b, GATE).then_inc(attn_gate_ready, 1)
                        pe.wait_ge(y_done, attn + 1)
                        transposes(attn_a, y).then_inc(y_t_ready, 1)
                    if b == at["ROUTER"] and prep is not None:
                        router(n + 1, 1 - odd)
                    if attn is not None and b == at["T_Z"]:
                        pe.wait_ge(attn_gate_done, attn + 1)
                        pe.wait_ge(y_norm_done, attn + 1)
                        transposes(attn_b, y_norm).then_inc(z_t_ready, 1)
                    if b == at["T_GATES"] and prep is not None:
                        gates_transpose(n + 1)
                    if attn is not None and b == at["OUTPUT"]:
                        pe.wait_ge(z_lo_done, attn + 1)
                        product(attn_a[:], attn_w_hi[:, OUT, :], attn_w_lo[:, OUT, :], z_hi[:],
                                z_lo[:]).then_inc(attn_out_ready, 1)

            pe.wait_ge(ident_ready, 1)
            for _ in range(WARM_UP_PRODUCTS):
                nc.tensor.transpose(attn_b[:, 0:P], ident[:], ident[:])
            prep_transpose(0)
            run_slots(pe, slot)
            for b in range(BLOCKS - DOWN_LAG, BLOCKS):
                down(BLOCKS * (UNITS - 1) + b, b, UNITS - 1)
            resid_transpose(UNITS - 1)


_INS = ["L0_attn_x", "L0_attn_Wq", "L0_attn_Wv", "L0_attn_Wg", "L0_attn_Wo", "L0_attn_beta", "L0_attn_ln_gamma",
        "L0_attn_ln_beta", "L0_ffn_w_gate", "L0_ffn_w_g", "L0_ffn_w_u", "L0_ffn_w_d"]


def kernel(**inputs):
    import numpy as _np
    import concourse.bacc as _bacc
    from concourse import mybir as _mybir
    from concourse.bass_utils import run_bass_kernel_spmd as _run

    nc = _bacc.Bacc("TRN2", target_bir_lowering=False, num_devices=1)
    arrays, args = {}, []
    for name in _INS:
        a = _np.ascontiguousarray(inputs[name])
        arrays[f"in_{name}_dram"] = a
        args.append(nc.dram_tensor(f"in_{name}_dram", a.shape, _mybir.dt.from_np(a.dtype), kind="ExternalInput").ap())
    shape = inputs["L0_attn_x"].shape
    args.append(nc.dram_tensor("out_dram", shape, _mybir.dt.float32, kind="ExternalOutput").ap())
    macaron_kernel(nc, *args)
    r = _run(nc, [arrays], core_ids=[0])
    return r.results[0]["out_dram"]
```

```python
from contextlib import ExitStack

import concourse.bass as bass
from concourse import mybir

F32 = mybir.dt.float32
F32R = mybir.dt.float32r
U32 = mybir.dt.uint32
ACT = mybir.ActivationFunctionType
ALU = mybir.AluOpType

P = 128
LN_EPS = 1e-5
EULER = 2.718281828459045
GATES_DONE = 16
UNITS_AHEAD = 4
HI_LAG = 2
DOWN_LAG = 4
VALUE, QUERY, GATE, OUT = range(4)
SORTING = 6
WARM_UP_PRODUCTS = 30
WARM_UP_MORE = 8
WARM_UP = 3
FIRST_BLOCKS = 3
AT = dict(
    FIRST_UNIT=dict(FIRST_ROUTER=0, FIRST_TOP=0, FIRST_ROWS=0, FIRST_T_GATES=2, FIRST_GATES_COPY=2, DOWN_HI=1,
                    DOWN_LO=3, ATTN_W=7),
    RETENTION=dict(DOWN_COPY=4, T_DOWN=4, ADD_UNIT=5, STATS_P=1, SCALE_P=3, NORM_P=5, T_P=5, HI_P=6, LO_P=6,
                   ROUTER=6, TOP=7, EXP=7, GATE_ROWS=8, T_GATES=8, GATES_COPY=9, STATS_A=0, SCALE_A=0, NORM_A=2,
                   T_A=2, HI_A=2, LO_A=2, VALUE_QUERY=3, SCAN=3, GATE_Y=4, SILU_A=5, STATS_Y=5, SCALE_Y=5,
                   NORM_Y=7, T_Z=7, AFFINE=8, Z=8, Z_HI=10, Z_LO=10, OUTPUT=10, OUT_COPY=0, T_OUT=0, ADD_A=1),
    NO_RETENTION=dict(DOWN_COPY=4, T_DOWN=4, ADD_UNIT=5, STATS_P=2, SCALE_P=3, NORM_P=5, T_P=5, HI_P=6, LO_P=6,
                      ROUTER=6, TOP=7, EXP=7, GATE_ROWS=8, T_GATES=9, GATES_COPY=10, OUT_COPY=0, T_OUT=0,
                      ADD_A=1),
)


def macaron_kernel(nc, x_in, w_q, w_v, w_gate_attn, w_o, beta, ln_gamma, ln_beta, w_router, w_g, w_u, w_d, out):
    GROUPS, TOKENS, D = x_in.shape
    EXPERTS, _, HIDDEN = w_g.shape
    HEADS = beta.shape[0]
    TILES = TOKENS // P
    BLOCKS = EXPERTS * HIDDEN // P
    PER_EXPERT = P // EXPERTS
    UNITS = 2 * GROUPS
    HEAD_DIM = D // HEADS
    assert D == P and HIDDEN == PER_EXPERT * BLOCKS and TOKENS == 512

    def final_unit(g):
        return UNITS_AHEAD + 2 * g if g < GROUPS - UNITS_AHEAD else GROUPS + g

    def p_is(p, number):
        return isinstance(p, int) and p == number

    def half(h):
        return slice(h * TOKENS // 2, (h + 1) * TOKENS // 2)

    def wait(eng, sem, count):
        if not isinstance(count, int) or count > 0:
            eng.wait_ge(sem, count)

    with ExitStack() as ctx:
        def sb(name, shape, dt=F32):
            return ctx.enter_context(nc.sbuf_tensor(name, shape, dt))

        def bank(name):
            return ctx.enter_context(nc.psum_tensor(name, [P, 512], F32))

        def sem(name):
            return ctx.enter_context(nc.semaphore(name))

        x = sb("x", [P, GROUPS * TOKENS])

        gate_raw = sb("gate_raw", [P, EXPERTS * HIDDEN])
        up_raw = sb("up_raw", [P, EXPERTS * HIDDEN])
        down_raw = sb("down_raw", [P, EXPERTS * HIDDEN])
        gate_hi, gate_lo, up_hi, up_lo, down_hi, down_lo = (
            sb(n, [P, BLOCKS, P], F32R) for n in ("gate_hi", "gate_lo", "up_hi", "up_lo", "down_hi", "down_lo"))
        router_raw = sb("router_raw", [P, EXPERTS])
        router_split = sb("router_split", [P, 2 * EXPERTS], F32R)
        attn_raw = sb("attn_raw", [P, 4, P])
        attn_w_hi = sb("attn_w_hi", [P, 4, P], F32R)
        attn_w_lo = sb("attn_w_lo", [P, 4, P], F32R)
        beta_col = sb("beta_col", [P, 1])
        decay = sb("decay", [P, 1])
        gamma_col = sb("gamma_col", [P, 1])
        shift_col = sb("shift_col", [P, 1])

        ident = sb("ident", [P, P])
        minus_half = sb("minus_half", [P, TILES])
        euler = sb("euler", [P, TILES])
        expert_id = sb("expert_id", [P, EXPERTS])

        act_pulse = sb("act_pulse", [P, 5])
        dve_pulse = sb("dve_pulse", [P, 7])

        xt_hi = [sb(f"xt_hi{i}", [P, TOKENS], F32R) for i in range(2)]
        xt_lo = [sb(f"xt_lo{i}", [P, TOKENS], F32R) for i in range(2)]
        gates = [sb(f"gates{i}", [P, TOKENS]) for i in range(2)]
        silu = sb("silu", [P, 2, TOKENS])
        hidden = sb("hidden", [P, BLOCKS, TOKENS])
        hidden_hi = sb("hidden_hi", [P, BLOCKS, TOKENS], F32R)
        hidden_lo = sb("hidden_lo", [P, BLOCKS, TOKENS], F32R)
        half_down = sb("half_down", [P, TOKENS])

        prep_xn = sb("prep_xn", [P, TOKENS])
        prep_bn = sb("prep_bn", [P, TILES, 6])
        prep_mv = sb("prep_mv", [P, TILES, 2])
        prep_ve = sb("prep_ve", [P, TILES])
        prep_nm = sb("prep_nm", [P, TILES])
        prep_rstd = sb("prep_rstd", [P, TILES])
        prep_bias = sb("prep_bias", [P, TILES])
        scores = sb("scores", [P, TILES, EXPERTS])
        scores_half = sb("scores_half", [P, TILES, EXPERTS])
        sorted_scores = sb("sorted_scores", [P, TILES, 8])
        sorted_ids = sb("sorted_ids", [P, TILES, 8], U32)
        top_ids = sb("top_ids", [P, TILES, 2])
        is_top = sb("is_top", [P, TILES, 2, EXPERTS])
        top_gap = sb("top_gap", [P, TILES])
        top_exp = sb("top_exp", [P, TILES])
        top_sum = sb("top_sum", [P, TILES])
        top_prob = sb("top_prob", [P, TILES, 2])
        top_gate = sb("top_gate", [P, TILES, 2, EXPERTS])
        gates_tok = sb("gates_tok", [P, EXPERTS, TILES])
        gates_row = sb("gates_row", [EXPERTS * TILES, P])
        first_gates_tok = sb("first_gates_tok", [P, TILES, EXPERTS, PER_EXPERT])

        attn_xn = sb("attn_xn", [P, TOKENS])
        attn_bn = sb("attn_bn", [P, TILES, 6])
        attn_mv = sb("attn_mv", [P, TILES, 2])
        attn_ve = sb("attn_ve", [P, TILES])
        attn_nm = sb("attn_nm", [P, TILES])
        attn_rstd = sb("attn_rstd", [P, TILES])
        attn_bias = sb("attn_bias", [P, TILES])
        attn_xt_hi = sb("attn_xt_hi", [P, TOKENS], F32R)
        attn_xt_lo = sb("attn_xt_lo", [P, TOKENS], F32R)
        state = sb("state", [P, TOKENS])
        y = sb("y", [P, TOKENS])
        y_bn = sb("y_bn", [P, TILES, 6])
        y_mv = sb("y_mv", [P, TILES, 2])
        y_ve = sb("y_ve", [P, TILES])
        y_nm = sb("y_nm", [P, TILES])
        y_rstd = sb("y_rstd", [P, TILES])
        y_bias = sb("y_bias", [P, TILES])
        y_norm = sb("y_norm", [P, TOKENS])
        attn_gate = sb("attn_gate", [P, TOKENS])
        z_affine = sb("z_affine", [P, TOKENS])
        z = sb("z", [P, TOKENS])
        z_hi = sb("z_hi", [P, TOKENS], F32R)
        z_lo = sb("z_lo", [P, TOKENS], F32R)
        attn_out = sb("attn_out", [P, TOKENS])

        gate_ps = [bank(f"gate_ps{i}") for i in range(2)]
        up_ps = [bank(f"up_ps{i}") for i in range(2)]
        down_ps = bank("down_ps")
        prep_ps = bank("prep_ps")
        attn_a = bank("attn_a")
        attn_b = bank("attn_b")

        gates_dram = nc.dram_tensor("gates_dram", (EXPERTS, TOKENS), F32, kind="Internal").ap()

        x0_loaded = sem("x0_loaded")
        x_loaded = sem("x_loaded")
        router_loaded = sem("router_loaded")
        gate_loaded = sem("gate_loaded")
        up_loaded = sem("up_loaded")
        down_loaded = sem("down_loaded")
        attn_loaded = sem("attn_loaded")
        beta_loaded = sem("beta_loaded")
        columns_loaded = sem("columns_loaded")
        ident_zero = sem("ident_zero")
        ident_ready = sem("ident_ready")
        consts_ready = sem("consts_ready")
        router_hi_ready = sem("router_hi_ready")
        router_ready = sem("router_ready")
        gate_w_hi_ready = sem("gate_w_hi_ready")
        up_w_hi_ready = sem("up_w_hi_ready")
        down_w_hi_ready = sem("down_w_hi_ready")
        gate_w_ready = sem("gate_w_ready")
        gate_w_rest_ready = sem("gate_w_rest_ready")
        up_w_ready = sem("up_w_ready")
        down_w_ready = sem("down_w_ready")
        decay_ready = sem("decay_ready")
        attn_wt_ready = sem("attn_wt_ready")
        attn_w_hi_ready = sem("attn_w_hi_ready")
        attn_w_ready = sem("attn_w_ready")
        gate_ready = sem("gate_ready")
        up_ready = sem("up_ready")
        silu_done = sem("silu_done")
        product_done = sem("product_done")
        gated_done = sem("gated_done")
        hidden_hi_done = sem("hidden_hi_done")
        hidden_lo_done = sem("hidden_lo_done")
        down_done = sem("down_done")
        down_copied = sem("down_copied")
        resid_t_ready = sem("resid_t_ready")
        resid_done = sem("resid_done")
        prep_bn_done = sem("prep_bn_done")
        prep_mv_done = sem("prep_mv_done")
        prep_stats_done = sem("prep_stats_done")
        prep_rstd_done = sem("prep_rstd_done")
        prep_scale_done = sem("prep_scale_done")
        prep_norm_done = sem("prep_norm_done")
        prep_t_ready = sem("prep_t_ready")
        prep_hi_done = sem("prep_hi_done")
        prep_lo_done = sem("prep_lo_done")
        scores_ready = sem("scores_ready")
        scores_half_copied = sem("scores_half_copied")
        scores_copied = sem("scores_copied")
        sorted_done = sem("sorted_done")
        ids_done = sem("ids_done")
        gap_done = sem("gap_done")
        exp_done = sem("exp_done")
        top_ids_done = sem("top_ids_done")
        is_top_done = sem("is_top_done")
        sum_done = sem("sum_done")
        first_prob_done = sem("first_prob_done")
        probs_done = sem("probs_done")
        top_gate_done = sem("top_gate_done")
        gates_tok_done = sem("gates_tok_done")
        gates_t_ready = sem("gates_t_ready")
        gates_copied = sem("gates_copied")
        gates_stored = sem("gates_stored")
        gates_done = sem("gates_done")
        attn_bn_done = sem("attn_bn_done")
        attn_mv_done = sem("attn_mv_done")
        attn_stats_done = sem("attn_stats_done")
        attn_rstd_done = sem("attn_rstd_done")
        attn_scale_done = sem("attn_scale_done")
        attn_norm_done = sem("attn_norm_done")
        attn_t_ready = sem("attn_t_ready")
        attn_hi_done = sem("attn_hi_done")
        attn_lo_done = sem("attn_lo_done")
        value_ready = sem("value_ready")
        query_ready = sem("query_ready")
        attn_gate_ready = sem("attn_gate_ready")
        state_done = sem("state_done")
        attn_gate_done = sem("attn_gate_done")
        y_done = sem("y_done")
        y_t_ready = sem("y_t_ready")
        y_bn_done = sem("y_bn_done")
        y_mv_done = sem("y_mv_done")
        y_stats_done = sem("y_stats_done")
        y_rstd_done = sem("y_rstd_done")
        y_scale_done = sem("y_scale_done")
        y_norm_done = sem("y_norm_done")
        z_t_ready = sem("z_t_ready")
        z_affine_done = sem("z_affine_done")
        z_done = sem("z_done")
        z_hi_done = sem("z_hi_done")
        z_lo_done = sem("z_lo_done")
        attn_out_ready = sem("attn_out_ready")
        attn_out_copied = sem("attn_out_copied")
        attn_resid_t_ready = sem("attn_resid_t_ready")
        attn_resid_done = sem("attn_resid_done")
        stored = sem("stored")

        def run_slots(eng, slot):
            slot(n=0, odd=0, prep=1)
            slot(n=1, odd=1, prep=2, done=0)
            with eng.Fori(0, 4) as i:
                first = 1 // (i + 1)
                why = "i is in 0..3"
                even_done = nc.s_assert_within((i + 2) - first, 1, 5, skip_runtime_bounds_check_because=why)
                odd_done = nc.s_assert_within((i + 3 * first) - 1, 0, 2, skip_runtime_bounds_check_because=why)
                slot(n=2 * i + 2, odd=0, prep=i + 3, attn=i, done=even_done)
                slot(n=2 * i + 3, odd=1, prep=i, left=i, done=odd_done)
            slot(n=10, odd=0, prep=7, attn=4, done=6)
            slot(n=11, odd=1, prep=4, attn=5, left=4, done=3)
            slot(n=12, odd=0, prep=5, attn=6, left=5, done=7)
            slot(n=13, odd=1, prep=6, attn=7, left=6, done=4)
            slot(n=14, odd=0, prep=7, left=7, done=5)
            slot(n=15, odd=1, done=6)

        gate_source = gate_raw[:].rearrange("k (p b) -> k b p", b=BLOCKS)
        up_source = up_raw[:].rearrange("k (p b) -> k b p", b=BLOCKS)
        down_source = down_raw[:].rearrange("k (b d) -> k b d", b=BLOCKS)

        block = ctx.enter_context(nc.Block())

        @block.sync
        def _(sp):
            xv = x[:].rearrange("p (g t d) -> p g t d", t=TILES, d=D)
            sp.dma_start(xv[:, 0], x_in[0].rearrange("(t p) d -> p t d", p=P)).then_inc(x0_loaded, 16)
            sp.dma_start(gate_raw[:].rearrange("d (e m) -> d e m", e=EXPERTS),
                         w_g.rearrange("e d m -> d e m")).then_inc(gate_loaded, 16)
            sp.dma_start(up_raw[:].rearrange("d (e m) -> d e m", e=EXPERTS),
                         w_u.rearrange("e d m -> d e m")).then_inc(up_loaded, 16)
            sp.dma_start(down_raw[:], w_d.rearrange("e m d -> (e m) d").rearrange(
                "(p b) d -> p (b d)", b=BLOCKS)).then_inc(down_loaded, 16)
            for g in range(1, GROUPS):
                sp.dma_start(xv[:, g], x_in[g].rearrange("(t p) d -> p t d", p=P)).then_inc(x_loaded, 16)
            for k, w in ((VALUE, w_v), (QUERY, w_q), (GATE, w_gate_attn), (OUT, w_o)):
                sp.dma_start(attn_raw[:, k, :], w).then_inc(attn_loaded, 16)
            sp.dma_start(gamma_col[:], ln_gamma.rearrange("(d o) -> d o", o=1)).then_inc(columns_loaded, 16)
            sp.dma_start(shift_col[:], ln_beta.rearrange("(d o) -> d o", o=1)).then_inc(columns_loaded, 16)

            def store(g):
                sp.wait_ge(resid_done, final_unit(g) + 1)
                sp.dma_start(out[g].rearrange("(t p) d -> p t d", p=P), xv[:, g]).then_inc(stored, 16)

            for unit in range(1, UNITS):
                sp.wait_ge(gates_copied, unit)
                sp.wait_ge(gates_done, GATES_DONE * unit)
                sp.dma_start(gates_dram.rearrange("e (t q) -> (e t) q", t=TILES),
                             gates_row[:]).then_inc(gates_stored, 16)
                sp.wait_ge(gates_stored, 16 * unit)
                wait(sp, gated_done, BLOCKS * (unit - 1))
                sp.dma_start(gates[unit % 2][:], gates_dram.unsqueeze(1).broadcast_to(
                    [EXPERTS, PER_EXPERT, TOKENS])).then_inc(gates_done, GATES_DONE)
                for g in range(GROUPS):
                    if final_unit(g) == unit - 2:
                        store(g)
            for g in range(GROUPS):
                if final_unit(g) == UNITS - 2:
                    store(g)
            for h in range(2):
                sp.wait_ge(resid_done, UNITS + h)
                tiles = slice(h * TILES // 2, (h + 1) * TILES // 2)
                sp.dma_start(out[GROUPS - 1].rearrange("(t p) d -> p t d", p=P)[:, tiles],
                             xv[:, GROUPS - 1, tiles]).then_inc(stored, 16)
            sp.wait_ge(stored, 16 * (GROUPS + 1))

        @block.gpsimd
        def _(pool):
            nc.gpsimd.memset(ident[:], 0.0).then_inc(ident_zero, 1)
            pool.wait_ge(ident_zero, 1)
            nc.gpsimd.affine_select(out=ident[:], in_=ident[:], compare_op=ALU.not_equal, fill=1.0, base=0,
                                    pattern=[[-1, P]], channel_multiplier=1).then_inc(ident_ready, 1)
            nc.gpsimd.memset(minus_half[:], -0.5)
            nc.gpsimd.memset(euler[:], EULER)
            for e in range(EXPERTS):
                last = nc.gpsimd.memset(expert_id[:, e:e + 1], float(e))
            last.then_inc(consts_ready, 1)
            pool.wait_ge(consts_ready, 1)

            def scale_of(ve, nm, rstd, bias, stats_done, rstd_done, scale_done, count):
                pool.wait_ge(stats_done, count)
                nc.gpsimd.tensor_tensor(rstd[:], ve[:], minus_half[:], ALU.pow).then_inc(rstd_done, 1)
                pool.wait_ge(rstd_done, count)
                nc.gpsimd.tensor_tensor(bias[:], nm[:], rstd[:], ALU.mult).then_inc(scale_done, 1)

            def prep_scale(p):
                scale_of(prep_ve, prep_nm, prep_rstd, prep_bias, prep_stats_done, prep_rstd_done,
                         prep_scale_done, p + 1)

            def top_exponential(p):
                pool.wait_ge(gap_done, p + 1)
                nc.gpsimd.tensor_tensor(top_exp[:], euler[:], top_gap[:], ALU.pow).then_inc(exp_done, 1)

            def slot(n, odd, prep=None, attn=None, left=None, done=None):
                at = AT["NO_RETENTION" if attn is None else "RETENTION"]
                for b in range(BLOCKS):
                    if attn is not None and b == at["SCALE_A"]:
                        scale_of(attn_ve, attn_nm, attn_rstd, attn_bias, attn_stats_done, attn_rstd_done,
                                 attn_scale_done, attn + 1)
                    if b == at["SCALE_P"] and prep is not None:
                        prep_scale(n + 1)
                    if attn is not None and b == at["SCALE_Y"]:
                        scale_of(y_ve, y_nm, y_rstd, y_bias, y_stats_done, y_rstd_done, y_scale_done, attn + 1)
                    if b == at["EXP"] and prep is not None:
                        top_exponential(n + 1)
                    if attn is not None and b == at["Z"]:
                        pool.wait_ge(z_affine_done, attn + 1)
                        pool.wait_ge(attn_gate_done, attn + 1)
                        nc.gpsimd.tensor_tensor(z[:], z_affine[:], attn_gate[:], ALU.mult).then_inc(z_done, 1)
                    if b == 0:
                        pool.wait_ge(gates_done, GATES_DONE * (n + 1))
                    pool.wait_ge(product_done, BLOCKS * n + b + 1)
                    nc.gpsimd.tensor_tensor(hidden[:, b, :], hidden[:, b, :], gates[odd][:],
                                            ALU.mult).then_inc(gated_done, 1)

            prep_scale(0)
            rest = slice(FIRST_BLOCKS, BLOCKS)
            pool.wait_ge(gate_w_hi_ready, 2)
            nc.gpsimd.tensor_tensor(gate_lo[:, rest, :], gate_source[:, rest, :], gate_hi[:, rest, :].bitcast(F32),
                                    ALU.subtract).then_inc(gate_w_rest_ready, 1)
            top_exponential(0)
            run_slots(pool, slot)

        @block.scalar
        def _(act):
            act.dma_start(beta_col[:], beta.rearrange("(h o) -> h o", o=1).broadcast_to(
                [HEADS, HEAD_DIM])).then_inc(beta_loaded, 16)
            act.dma_start(router_raw[:], w_router).then_inc(router_loaded, 16)
            act.wait_ge(consts_ready, 1)
            nc.scalar.activation(act_pulse[:, WARM_UP:WARM_UP + 1], minus_half[:, 0:1], ACT.Sigmoid)
            act.wait_ge(beta_loaded, 16)
            nc.scalar.activation(decay[:], beta_col[:], ACT.Sigmoid).then_inc(decay_ready, 1)
            nc.scalar.activation(act_pulse[:, WARM_UP + 1:WARM_UP + 2], minus_half[:, 0:1], ACT.Silu)

            def normalise(dst, src_tile, rstd, bias, scale_done, norm_done, count, pulse):
                act.wait_ge(scale_done, count)
                nc.scalar.activation(act_pulse[:, pulse:pulse + 1], minus_half[:, 0:1], ACT.Copy)
                for t in range(TILES):
                    last = nc.scalar.activation(dst[:, t * P:(t + 1) * P], src_tile(t), ACT.Identity,
                                                bias=bias[:, t:t + 1], scale=rstd[:, t:t + 1])
                last.then_inc(norm_done, 1)

            def prep_norm(p, g):
                wait(act, prep_t_ready, p)
                normalise(prep_xn, lambda t: x[:, bass.ds(g * TOKENS + t * P, P)], prep_rstd, prep_bias,
                          prep_scale_done, prep_norm_done, p + 1, pulse=0)

            def prep_hi(p, odd):
                act.wait_ge(prep_t_ready, p + 1)
                nc.scalar.activation(xt_hi[odd][:], prep_ps[:], ACT.Copy).then_inc(prep_hi_done, 1)

            def first_gates_copy():
                act.wait_ge(gates_t_ready, 1)
                nc.scalar.activation(gates[0][:], prep_ps[:], ACT.Copy).then_inc(gates_done, GATES_DONE)

            def gates_copy(p):
                act.wait_ge(gates_t_ready, p + 1)
                wait(act, gates_stored, 16 * (p - 1))
                nc.scalar.activation(gates_row[:], prep_ps[0:TILES * EXPERTS, 0:P], ACT.Copy).then_inc(gates_copied, 1)

            def weight_hi(hi, source, blocks, ready):
                nc.scalar.activation(hi[:, blocks, :], source[:, blocks, :], ACT.Copy).then_inc(ready, 1)

            def hidden_split(q, b):
                act.wait_ge(gated_done, q + 1)
                wait(act, down_done, q + 1 - BLOCKS)
                nc.scalar.activation(hidden_hi[:, b, :], hidden[:, b, :], ACT.Copy).then_inc(hidden_hi_done, 1)

            def copy_down(n):
                act.wait_ge(down_done, BLOCKS * (n + 1))
                wait(act, resid_t_ready, n)
                nc.scalar.activation(half_down[:], down_ps[:], ACT.Copy, scale=0.5).then_inc(down_copied, 1)

            def slot(n, odd, prep=None, attn=None, left=None, done=None):
                at = AT["NO_RETENTION" if attn is None else "RETENTION"]
                for b in range(BLOCKS):
                    if b == at["OUT_COPY"] and left is not None:
                        act.wait_ge(attn_out_ready, left + 1)
                        nc.scalar.activation(attn_out[:], attn_a[:], ACT.Copy).then_inc(attn_out_copied, 1)
                    if attn is not None and b == at["NORM_A"]:
                        wait(act, attn_t_ready, attn)
                        normalise(attn_xn, lambda t: x[:, bass.ds(attn * TOKENS + t * P, P)], attn_rstd, attn_bias,
                                  attn_scale_done, attn_norm_done, attn + 1, pulse=1)
                    if b == at["DOWN_COPY"] and done is not None:
                        copy_down(n - 1)
                    if attn is not None and b == at["HI_A"]:
                        act.wait_ge(attn_t_ready, attn + 1)
                        nc.scalar.activation(attn_xt_hi[:], attn_a[:], ACT.Copy).then_inc(attn_hi_done, 1)
                    if b == at["NORM_P"] and prep is not None:
                        prep_norm(n + 1, prep)
                    if b == at["HI_P"] and prep is not None:
                        prep_hi(n + 1, 1 - odd)
                    if attn is not None and b == at["SILU_A"]:
                        act.wait_ge(attn_gate_ready, attn + 1)
                        nc.scalar.activation(attn_gate[:], attn_b[:], ACT.Silu).then_inc(attn_gate_done, 1)
                    if attn is not None and b == at["NORM_Y"]:
                        normalise(y_norm, lambda t: attn_a[:, t * P:(t + 1) * P], y_rstd, y_bias,
                                  y_scale_done, y_norm_done, attn + 1, pulse=2)
                    if attn is not None and b == at["AFFINE"]:
                        act.wait_ge(z_t_ready, attn + 1)
                        nc.scalar.activation(z_affine[:], attn_b[:], ACT.Identity, bias=shift_col[:, 0:1],
                                             scale=gamma_col[:, 0:1]).then_inc(z_affine_done, 1)
                    if b == at["GATES_COPY"] and prep is not None:
                        gates_copy(n + 1)
                    if attn is not None and b == at["Z_HI"]:
                        act.wait_ge(z_done, attn + 1)
                        nc.scalar.activation(z_hi[:], z[:], ACT.Copy).then_inc(z_hi_done, 1)
                    if isinstance(n, int) and n == 0 and b == AT["FIRST_UNIT"]["DOWN_HI"]:
                        act.wait_ge(down_loaded, 16)
                        weight_hi(down_hi, down_source, slice(0, BLOCKS), down_w_hi_ready)
                    if isinstance(n, int) and n == 0 and b == AT["FIRST_UNIT"]["FIRST_GATES_COPY"]:
                        first_gates_copy()
                    if isinstance(n, int) and n == 0 and b == AT["FIRST_UNIT"]["ATTN_W"]:
                        act.wait_ge(columns_loaded, 32)
                        act.wait_ge(attn_wt_ready, 1)
                        nc.scalar.activation(attn_w_hi[:].rearrange("p k c -> p (k c)"), attn_a[:],
                                             ACT.Copy).then_inc(attn_w_hi_ready, 1)
                    q = BLOCKS * n + b
                    act.wait_ge(gate_ready, q + 1)
                    wait(act, product_done, q - 1)
                    nc.scalar.activation(silu[:, (odd + b) % 2, :], gate_ps[(odd + b) % 2][:],
                                         ACT.Silu).then_inc(silu_done, 1)
                    if not isinstance(n, int) or n > 0 or b >= HI_LAG:
                        hidden_split(q - HI_LAG, (b - HI_LAG) % BLOCKS)

            act.wait_ge(router_loaded, 16)
            nc.scalar.activation(router_split[:, 0:EXPERTS], router_raw[:], ACT.Copy).then_inc(router_hi_ready, 1)
            first, rest = slice(0, FIRST_BLOCKS), slice(FIRST_BLOCKS, BLOCKS)
            act.wait_ge(gate_loaded, 16)
            weight_hi(gate_hi, gate_source, first, gate_w_hi_ready)
            weight_hi(gate_hi, gate_source, rest, gate_w_hi_ready)
            act.wait_ge(up_loaded, 16)
            weight_hi(up_hi, up_source, first, up_w_hi_ready)
            prep_hi(0, 0)
            weight_hi(up_hi, up_source, rest, up_w_hi_ready)
            run_slots(act, slot)
            for b in range(BLOCKS - HI_LAG, BLOCKS):
                hidden_split(BLOCKS * (UNITS - 1) + b, b)
            act.wait_ge(down_done, BLOCKS * UNITS)
            act.wait_ge(resid_t_ready, UNITS - 1)
            for h in range(2):
                nc.scalar.activation(half_down[:, half(h)], down_ps[:, half(h)], ACT.Copy,
                                     scale=0.5).then_inc(down_copied, 1)

        @block.vector
        def _(dve):
            def stand_in(pulse):
                nc.vector.memset(dve_pulse[:, pulse:pulse + 1], 0.0)

            def moments(src_tile, bn, mv, ve, nm, bn_done, mv_done, stats_done, count, pulse):
                stand_in(pulse + 1)
                for t in range(TILES):
                    last = nc.vector.bn_stats(bn[:, t, :], src_tile(t))
                last.then_inc(bn_done, 1)
                dve.wait_ge(bn_done, count)
                stand_in(pulse)
                for t in range(TILES):
                    last = nc.vector.bn_aggr(mv[:, t, :], bn[:, t, :])
                last.then_inc(mv_done, 1)
                dve.wait_ge(mv_done, count)
                nc.vector.tensor_scalar(ve[:], mv[:, :, 1], LN_EPS, None, ALU.add)
                nc.vector.tensor_scalar(nm[:], mv[:, :, 0], -1.0, None, ALU.mult).then_inc(stats_done, 1)

            def prep_moments(p, g):
                moments(lambda t: x[:, bass.ds(g * TOKENS + t * P, P)], prep_bn, prep_mv, prep_ve, prep_nm,
                        prep_bn_done, prep_mv_done, prep_stats_done, p + 1, pulse=0)

            def prep_lo(p, odd):
                dve.wait_ge(prep_hi_done, p + 1)
                nc.vector.tensor_tensor(xt_lo[odd][:], prep_ps[:], xt_hi[odd][:].bitcast(F32),
                                        ALU.subtract).then_inc(prep_lo_done, 1)

            def top_two(p):
                dve.wait_ge(scores_ready, p + 1)
                halves = prep_ps[:, 0:2 * TILES * EXPERTS].rearrange("p (t h e) -> p t h e", h=2, e=EXPERTS)
                nc.vector.tensor_copy(scores_half[:], halves[:, :, 1, :]).then_inc(scores_half_copied, 1)
                dve.wait_ge(scores_half_copied, p + 1)
                nc.vector.tensor_tensor(scores[:], halves[:, :, 0, :], scores_half[:],
                                        ALU.add).then_inc(scores_copied, 1)
                dve.wait_ge(scores_copied, p + 1)
                stand_in(SORTING)
                for t in range(TILES):
                    last = nc.vector.max(sorted_scores[:, t, :], scores[:, t, :])
                last.then_inc(sorted_done, 1)
                dve.wait_ge(sorted_done, p + 1)
                nc.vector.tensor_tensor(top_gap[:], sorted_scores[:, :, 1], sorted_scores[:, :, 0],
                                        ALU.subtract).then_inc(gap_done, 1)
                for t in range(TILES):
                    last = nc.vector.max_index(sorted_ids[:, t, :], sorted_scores[:, t, :], scores[:, t, :])
                last.then_inc(ids_done, 1)
                dve.wait_ge(ids_done, p + 1)
                nc.vector.tensor_copy(top_ids[:], sorted_ids[:, :, 0:2]).then_inc(top_ids_done, 1)
                dve.wait_ge(top_ids_done, p + 1)
                shape = [P, TILES, 2, EXPERTS]
                nc.vector.tensor_tensor(is_top[:], expert_id[:].unsqueeze(1).unsqueeze(1).broadcast_to(shape),
                                        top_ids[:].unsqueeze(3).broadcast_to(shape),
                                        ALU.is_equal).then_inc(is_top_done, 1)

            def gate_rows(p):
                dve.wait_ge(exp_done, p + 1)
                nc.vector.tensor_scalar(top_sum[:], top_exp[:], 1.0, None, ALU.add).then_inc(sum_done, 1)
                dve.wait_ge(sum_done, p + 1)
                nc.vector.reciprocal(top_prob[:, :, 0], top_sum[:]).then_inc(first_prob_done, 1)
                dve.wait_ge(first_prob_done, p + 1)
                nc.vector.tensor_tensor(top_prob[:, :, 1], top_prob[:, :, 0], top_exp[:],
                                        ALU.mult).then_inc(probs_done, 1)
                dve.wait_ge(probs_done, p + 1)
                dve.wait_ge(is_top_done, p + 1)
                nc.vector.tensor_tensor(top_gate[:], is_top[:],
                                        top_prob[:].unsqueeze(3).broadcast_to([P, TILES, 2, EXPERTS]),
                                        ALU.mult).then_inc(top_gate_done, 1)
                dve.wait_ge(top_gate_done, p + 1)
                if p_is(p, 0):
                    shape = [P, TILES, EXPERTS, PER_EXPERT]
                    nc.vector.tensor_tensor(first_gates_tok[:], top_gate[:, :, 0, :].unsqueeze(3).broadcast_to(shape),
                                            top_gate[:, :, 1, :].unsqueeze(3).broadcast_to(shape),
                                            ALU.add).then_inc(gates_tok_done, 1)
                else:
                    nc.vector.tensor_tensor(gates_tok[:].rearrange("p e t -> p t e"), top_gate[:, :, 0, :],
                                            top_gate[:, :, 1, :],
                                            ALU.add).then_inc(gates_tok_done, 1)

            def weight_lo(hi, lo, source, blocks, ready):
                nc.vector.tensor_tensor(lo[:, blocks, :], source[:, blocks, :], hi[:, blocks, :].bitcast(F32),
                                        ALU.subtract).then_inc(ready, 1)

            def hidden_rest(q, b):
                dve.wait_ge(hidden_hi_done, q + 1)
                nc.vector.tensor_tensor(hidden_lo[:, b, :], hidden[:, b, :], hidden_hi[:, b, :].bitcast(F32),
                                        ALU.subtract).then_inc(hidden_lo_done, 1)

            def add_unit(n, g):
                dve.wait_ge(resid_t_ready, n + 1)
                xg = x[:, bass.ds(g * TOKENS, TOKENS)]
                nc.vector.tensor_tensor(xg, prep_ps[:], xg, ALU.add).then_inc(resid_done, 1)

            def slot(n, odd, prep=None, attn=None, left=None, done=None):
                at = AT["NO_RETENTION" if attn is None else "RETENTION"]
                for b in range(BLOCKS):
                    if attn is not None and b == at["STATS_A"]:
                        dve.wait_ge(resid_done, n - 1)
                        moments(lambda t: x[:, bass.ds(attn * TOKENS + t * P, P)], attn_bn, attn_mv, attn_ve, attn_nm,
                                attn_bn_done, attn_mv_done, attn_stats_done, attn + 1, pulse=2)
                    if b == at["ADD_A"] and left is not None:
                        dve.wait_ge(attn_resid_t_ready, left + 1)
                        xg = x[:, bass.ds(left * TOKENS, TOKENS)]
                        nc.vector.tensor_tensor(xg, attn_b[:], xg, ALU.add).then_inc(attn_resid_done, 1)
                    if b == at["STATS_P"] and prep is not None:
                        if isinstance(n, int) and n == 0:
                            dve.wait_ge(x_loaded, 16 * (GROUPS - 1))
                        if left is not None:
                            dve.wait_ge(attn_resid_done, left + 1)
                        prep_moments(n + 1, prep)
                    if attn is not None and b == at["LO_A"]:
                        dve.wait_ge(attn_hi_done, attn + 1)
                        nc.vector.tensor_tensor(attn_xt_lo[:], attn_a[:], attn_xt_hi[:].bitcast(F32),
                                                ALU.subtract).then_inc(attn_lo_done, 1)
                    if b == at["ADD_UNIT"] and done is not None:
                        add_unit(n - 1, done)
                    if attn is not None and b == at["SCAN"]:
                        dve.wait_ge(value_ready, attn + 1)
                        nc.vector.tensor_tensor_scan(state[:], decay[:, 0:1].to_broadcast([P, TOKENS]), attn_b[:],
                                                     0.0, ALU.mult, ALU.add).then_inc(state_done, 1)
                        dve.wait_ge(state_done, attn + 1)
                        dve.wait_ge(query_ready, attn + 1)
                        nc.vector.tensor_tensor(y[:], attn_a[:], state[:], ALU.mult).then_inc(y_done, 1)
                    if attn is not None and b == at["STATS_Y"]:
                        dve.wait_ge(y_t_ready, attn + 1)
                        moments(lambda t: attn_a[:, t * P:(t + 1) * P], y_bn, y_mv, y_ve, y_nm,
                                y_bn_done, y_mv_done, y_stats_done, attn + 1, pulse=4)
                    if b == at["LO_P"] and prep is not None:
                        prep_lo(n + 1, 1 - odd)
                    if b == at["TOP"] and prep is not None:
                        top_two(n + 1)
                    if b == at["GATE_ROWS"] and prep is not None:
                        gate_rows(n + 1)
                    if attn is not None and b == at["Z_LO"]:
                        dve.wait_ge(z_hi_done, attn + 1)
                        nc.vector.tensor_tensor(z_lo[:], z[:], z_hi[:].bitcast(F32),
                                                ALU.subtract).then_inc(z_lo_done, 1)
                    if isinstance(n, int) and n == 0:
                        if b == AT["FIRST_UNIT"]["FIRST_TOP"]:
                            top_two(0)
                        if b == AT["FIRST_UNIT"]["FIRST_ROWS"]:
                            gate_rows(0)
                        if b == AT["FIRST_UNIT"]["DOWN_LO"]:
                            dve.wait_ge(down_w_hi_ready, 1)
                            weight_lo(down_hi, down_lo, down_source, slice(0, BLOCKS), down_w_ready)
                        if b == AT["FIRST_UNIT"]["ATTN_W"]:
                            dve.wait_ge(attn_w_hi_ready, 1)
                            nc.vector.tensor_tensor(attn_w_lo[:].rearrange("p k c -> p (k c)"), attn_a[:],
                                                    attn_w_hi[:].rearrange("p k c -> p (k c)").bitcast(F32),
                                                    ALU.subtract).then_inc(attn_w_ready, 1)
                    q = BLOCKS * n + b
                    dve.wait_ge(silu_done, q + 1)
                    dve.wait_ge(up_ready, q + 1)
                    nc.vector.tensor_tensor(hidden[:, b, :], up_ps[(odd + b) % 2][:], silu[:, (odd + b) % 2, :],
                                            ALU.mult).then_inc(product_done, 1)
                    if not isinstance(n, int) or n > 0 or b >= HI_LAG:
                        hidden_rest(q - HI_LAG, (b - HI_LAG) % BLOCKS)

            dve.wait_ge(x0_loaded, 16)
            prep_moments(0, 0)
            dve.wait_ge(router_hi_ready, 1)
            nc.vector.tensor_tensor(router_split[:, EXPERTS:2 * EXPERTS], router_raw[:],
                                    router_split[:, 0:EXPERTS].bitcast(F32), ALU.subtract).then_inc(router_ready, 1)
            dve.wait_ge(prep_scale_done, 1)
            for t in range(TILES):
                last = nc.vector.tensor_scalar(prep_xn[:, t * P:(t + 1) * P], x[:, t * P:(t + 1) * P],
                                               prep_rstd[:, t:t + 1], prep_bias[:, t:t + 1], ALU.mult, ALU.add)
            last.then_inc(prep_norm_done, 1)
            first, rest = slice(0, FIRST_BLOCKS), slice(FIRST_BLOCKS, BLOCKS)
            dve.wait_ge(gate_w_hi_ready, 1)
            weight_lo(gate_hi, gate_lo, gate_source, first, gate_w_ready)
            prep_lo(0, 0)
            dve.wait_ge(up_w_hi_ready, 1)
            weight_lo(up_hi, up_lo, up_source, first, up_w_ready)
            dve.wait_ge(up_w_hi_ready, 2)
            weight_lo(up_hi, up_lo, up_source, rest, up_w_ready)
            dve.wait_ge(consts_ready, 1)
            dve.wait_ge(decay_ready, 1)
            run_slots(dve, slot)
            for b in range(BLOCKS - HI_LAG, BLOCKS):
                hidden_rest(BLOCKS * (UNITS - 1) + b, b)
            for h in range(2):
                dve.wait_ge(resid_t_ready, UNITS + h)
                xg = x[:, (GROUPS - 1) * TOKENS:GROUPS * TOKENS][:, half(h)]
                nc.vector.tensor_tensor(xg, (prep_ps, attn_a)[h][:, half(h)], xg, ALU.add).then_inc(resid_done, 1)

        @block.tensor
        def _(pe):
            def product(dst, w_hi, w_lo, v_hi, v_lo, start=True, stop=True):
                nc.tensor.matmul(dst, w_hi, v_hi, start=start, stop=False)
                nc.tensor.matmul(dst, w_hi, v_lo, start=False, stop=False)
                return nc.tensor.matmul(dst, w_lo, v_hi, start=False, stop=stop)

            def transposes(dst, src, tiles=range(TILES)):
                for t in tiles:
                    last = nc.tensor.transpose(dst[:, t * P:(t + 1) * P], src[:, t * P:(t + 1) * P], ident[:])
                return last

            def warm_up(products):
                for _ in range(products):
                    nc.tensor.transpose(attn_b[:, 0:P], ident[:], ident[:])

            def prep_transpose(p):
                if p_is(p, 1):
                    pe.wait_ge(gates_done, GATES_DONE)
                elif not p_is(p, 0):
                    pe.wait_ge(gates_copied, p - 1)
                wait(pe, resid_done, p - 1)
                pe.wait_ge(prep_norm_done, p + 1)
                transposes(prep_ps, prep_xn).then_inc(prep_t_ready, 1)

            def router(p, odd):
                pe.wait_ge(prep_lo_done, p + 1)
                for t in range(TILES):
                    cols = slice(t * P, (t + 1) * P)
                    dst = prep_ps[:, 2 * t * EXPERTS:2 * (t + 1) * EXPERTS]
                    nc.tensor.matmul(dst, xt_hi[odd][:, cols], router_split[:], start=True, stop=False)
                    last = nc.tensor.matmul(dst, xt_lo[odd][:, cols], router_split[:], start=False, stop=True)
                last.then_inc(scores_ready, 1)

            def gates_transpose(p):
                pe.wait_ge(scores_copied, p + 1)
                pe.wait_ge(gates_tok_done, p + 1)
                if p_is(p, 0):
                    transposes(prep_ps, first_gates_tok[:].rearrange("p t e r -> p (t e r)")).then_inc(gates_t_ready, 1)
                else:
                    nc.tensor.transpose(prep_ps[0:TILES * EXPERTS, 0:P], gates_tok[:].rearrange("p e t -> p (e t)"),
                                        ident[:]).then_inc(gates_t_ready, 1)

            def down(q, b, n):
                pe.wait_ge(hidden_lo_done, q + 1)
                if b == 0:
                    wait(pe, down_copied, n)
                product(down_ps[:], down_hi[:, b, :], down_lo[:, b, :], hidden_hi[:, b, :], hidden_lo[:, b, :],
                        start=b == 0, stop=b == BLOCKS - 1).then_inc(down_done, 1)

            def attn_product(dst, k):
                return product(dst[:], attn_w_hi[:, k, :], attn_w_lo[:, k, :], attn_xt_hi[:], attn_xt_lo[:])

            def resid_transpose(n):
                pe.wait_ge(gates_copied, n + 1)
                pe.wait_ge(down_copied, n + 1)
                transposes(prep_ps, half_down).then_inc(resid_t_ready, 1)

            def slot(n, odd, prep=None, attn=None, left=None, done=None):
                at = AT["NO_RETENTION" if attn is None else "RETENTION"]
                pe.wait_ge(prep_lo_done, n + 1)
                for b in range(BLOCKS):
                    q = BLOCKS * n + b
                    if isinstance(n, int) and n == 0:
                        if b == 0:
                            pe.wait_ge(gate_w_ready, 1)
                        if b == FIRST_BLOCKS:
                            pe.wait_ge(gate_w_rest_ready, 1)
                        if b == AT["FIRST_UNIT"]["FIRST_ROUTER"]:
                            pe.wait_ge(router_ready, 1)
                            router(0, 0)
                        if b == AT["FIRST_UNIT"]["FIRST_T_GATES"]:
                            gates_transpose(0)
                        if b == AT["FIRST_UNIT"]["ATTN_W"]:
                            pe.wait_ge(attn_loaded, 64)
                            transposes(attn_a, attn_raw[:].rearrange("p k c -> p (k c)")).then_inc(attn_wt_ready, 1)
                    wait(pe, silu_done, q - 1)
                    product(gate_ps[(odd + b) % 2][:], gate_hi[:, b, :], gate_lo[:, b, :],
                            xt_hi[odd][:], xt_lo[odd][:]).then_inc(gate_ready, 1)
                    if isinstance(n, int) and n == 0 and b == 0:
                        pe.wait_ge(up_w_ready, 1)
                    if isinstance(n, int) and n == 0 and b == FIRST_BLOCKS:
                        pe.wait_ge(up_w_ready, 2)
                    wait(pe, product_done, q - 1)
                    product(up_ps[(odd + b) % 2][:], up_hi[:, b, :], up_lo[:, b, :],
                            xt_hi[odd][:], xt_lo[odd][:]).then_inc(up_ready, 1)
                    if isinstance(n, int) and n == 0 and b == DOWN_LAG:
                        pe.wait_ge(down_w_ready, 1)
                    if isinstance(n, int) and n == 1 and b == 0:
                        pe.wait_ge(attn_w_ready, 1)
                    if not isinstance(n, int) or n > 0 or b >= DOWN_LAG:
                        down(q - DOWN_LAG, (b - DOWN_LAG) % BLOCKS, n)
                    if b == at["T_OUT"] and left is not None:
                        pe.wait_ge(attn_out_copied, left + 1)
                        transposes(attn_b, attn_out).then_inc(attn_resid_t_ready, 1)
                    if attn is not None and b == at["T_A"]:
                        wait(pe, attn_out_copied, attn)
                        pe.wait_ge(attn_norm_done, attn + 1)
                        transposes(attn_a, attn_xn).then_inc(attn_t_ready, 1)
                    if b == at["T_DOWN"] and done is not None:
                        resid_transpose(n - 1)
                    if attn is not None and b == at["VALUE_QUERY"]:
                        wait(pe, attn_resid_done, attn)
                        pe.wait_ge(attn_lo_done, attn + 1)
                        attn_product(attn_b, VALUE).then_inc(value_ready, 1)
                        attn_product(attn_a, QUERY).then_inc(query_ready, 1)
                    if b == at["T_P"] and prep is not None:
                        prep_transpose(n + 1)
                    if attn is not None and b == at["GATE_Y"]:
                        pe.wait_ge(state_done, attn + 1)
                        attn_product(attn_b, GATE).then_inc(attn_gate_ready, 1)
                        pe.wait_ge(y_done, attn + 1)
                        transposes(attn_a, y).then_inc(y_t_ready, 1)
                    if b == at["ROUTER"] and prep is not None:
                        router(n + 1, 1 - odd)
                    if attn is not None and b == at["T_Z"]:
                        pe.wait_ge(attn_gate_done, attn + 1)
                        pe.wait_ge(y_norm_done, attn + 1)
                        transposes(attn_b, y_norm).then_inc(z_t_ready, 1)
                    if b == at["T_GATES"] and prep is not None:
                        gates_transpose(n + 1)
                    if attn is not None and b == at["OUTPUT"]:
                        pe.wait_ge(z_lo_done, attn + 1)
                        product(attn_a[:], attn_w_hi[:, OUT, :], attn_w_lo[:, OUT, :], z_hi[:],
                                z_lo[:]).then_inc(attn_out_ready, 1)

            pe.wait_ge(ident_ready, 1)
            warm_up(WARM_UP_PRODUCTS)
            prep_transpose(0)
            warm_up(WARM_UP_MORE)
            run_slots(pe, slot)
            for b in range(BLOCKS - DOWN_LAG, BLOCKS):
                down(BLOCKS * (UNITS - 1) + b, b, UNITS - 1)
            pe.wait_ge(gates_copied, UNITS - 1)
            for h in range(2):
                pe.wait_ge(down_copied, UNITS + h)
                transposes((prep_ps, attn_a)[h], half_down, range(h * TILES // 2, (h + 1) * TILES // 2)).then_inc(
                    resid_t_ready, 1)


_INS = ["L0_attn_x", "L0_attn_Wq", "L0_attn_Wv", "L0_attn_Wg", "L0_attn_Wo", "L0_attn_beta", "L0_attn_ln_gamma",
        "L0_attn_ln_beta", "L0_ffn_w_gate", "L0_ffn_w_g", "L0_ffn_w_u", "L0_ffn_w_d"]


def kernel(**inputs):
    import numpy as _np
    import concourse.bacc as _bacc
    from concourse import mybir as _mybir
    from concourse.bass_utils import run_bass_kernel_spmd as _run

    nc = _bacc.Bacc("TRN2", target_bir_lowering=False, num_devices=1)
    arrays, args = {}, []
    for name in _INS:
        a = _np.ascontiguousarray(inputs[name])
        arrays[f"in_{name}_dram"] = a
        args.append(nc.dram_tensor(f"in_{name}_dram", a.shape, _mybir.dt.from_np(a.dtype), kind="ExternalInput").ap())
    shape = inputs["L0_attn_x"].shape
    args.append(nc.dram_tensor("out_dram", shape, _mybir.dt.float32, kind="ExternalOutput").ap())
    macaron_kernel(nc, *args)
    r = _run(nc, [arrays], core_ids=[0])
    return r.results[0]["out_dram"]
```
